# Optimizing a Trainium2 kernel written in Bass

```python
import numpy as np
import jax
import jax.numpy as jnp

def _softmax(x, axis=-1):
    return jax.nn.softmax(x, axis=axis)

def _gelu(x):
    return jax.nn.gelu(x, approximate=True)

def _silu(x):
    return jax.nn.silu(x)

def _sigmoid(x):
    return jax.nn.sigmoid(x)

def _layernorm(x, axis=-1, eps=1e-05):
    m = jnp.mean(x, axis=axis, keepdims=True)
    v = jnp.var(x, axis=axis, keepdims=True)
    return (x - m) / jnp.sqrt(v + eps)

def _scatter_add(tgt, idx, src, axis=0):
    return tgt.at[idx].add(src)

def _segment_sum(src, seg, n):
    return jax.ops.segment_sum(src, seg, n)
kernel_name = 'mk_gnn_preln_d1_gnn_r8_8a60b8'

def setup_inputs(seed: int=0):
    np.random.seed(seed)
    _w = jnp.asarray

    def _rec_inputs():
        import jax
        import jax.numpy as jnp
        _gk = jax.random.key(seed)
        x = -0.0003713 + 1 * jax.random.normal(jax.random.fold_in(_gk, 1), (6250, 128), jnp.float32)
        src = jax.random.randint(jax.random.fold_in(_gk, 2), (100000,), 0, 6250, jnp.int32)
        dst = jnp.minimum((6250 * jax.random.uniform(jax.random.fold_in(_gk, 3), (100000,)) ** 2.0).astype(jnp.int32), 49999)
        _o = jnp.argsort(dst, stable=True)
        src = src[_o]
        dst = dst[_o]
        edge_attr_128 = -4.21973e-05 + 0.999841 * jax.random.normal(jax.random.fold_in(_gk, 12), (100000, 128), jnp.float32)
        return (x, src, dst, edge_attr_128)
    x, src, dst, edge_attr_128 = _rec_inputs()

    def _L0_gnn_setup():
        import jax, jax.numpy as jnp
        import numpy as np
        N_NODES = 12500
        N_EDGES = 75000
        D = 128
        key = jax.random.key(seed)
        ks = jax.random.split(key, 6)
        node_feat = jax.random.normal(ks[0], (N_NODES, D), dtype=jnp.float32)
        edge_feat = jax.random.normal(ks[1], (N_EDGES, D), dtype=jnp.float32)
        src = jax.random.randint(ks[2], (N_EDGES,), 0, N_NODES, dtype=jnp.int32)
        dst = jax.random.randint(ks[3], (N_EDGES,), 0, N_NODES, dtype=jnp.int32)
        lim = 1.0 / np.sqrt(D)
        W1 = jax.random.uniform(ks[4], (D, D), jnp.float32, -lim, lim)
        b1 = jnp.zeros((D,), jnp.float32)
        W2 = jax.random.uniform(ks[5], (D, D), jnp.float32, -lim, lim)
        b2 = jnp.zeros((D,), jnp.float32)
        return {'node_feat': node_feat, 'edge_feat': edge_feat, 'src': src, 'dst': dst, 'W1': W1, 'b1': b1, 'W2': W2, 'b2': b2}
    _L0_gnn_all = _L0_gnn_setup()
    _L0_gnn_in = {k: v for k, v in _L0_gnn_all.items() if k in ('W1', 'b1', 'W2', 'b2')}
    del _L0_gnn_all
    return {'x': x, 'src': src, 'dst': dst, 'edge_attr_128': edge_attr_128, 'L0_gnn_W1': _L0_gnn_in['W1'], 'L0_gnn_b1': _L0_gnn_in['b1'], 'L0_gnn_W2': _L0_gnn_in['W2'], 'L0_gnn_b2': _L0_gnn_in['b2']}

def reference(x, src, dst, edge_attr_128, L0_gnn_W1, L0_gnn_b1, L0_gnn_W2, L0_gnn_b2):
    import jax
    import jax.numpy as jnp

    def _L0_gnn_ref(node_feat, edge_feat, src, dst, W1, b1, W2, b2):
        import jax, jax.numpy as jnp
        import numpy as np
        N_NODES = 12500
        N_EDGES = 75000
        D = 128
        m = node_feat[src] + edge_feat
        neigh = jax.ops.segment_sum(m, dst, num_segments=node_feat.shape[0])
        h = 2.0 * node_feat + neigh
        h = h @ W1 + b1
        h = jnp.where(h > 0, h, 0.01 * h)
        return h @ W2 + b2
    h = jnp.maximum(_layernorm(x, axis=-1), 0.0)
    x = x + _L0_gnn_ref(h, edge_attr_128, src, dst, L0_gnn_W1, L0_gnn_b1, L0_gnn_W2, L0_gnn_b2)
    return x

_drawn_inputs = setup_inputs


def setup_inputs(seed=0):
    import zlib

    import numpy as np

    out = dict(_drawn_inputs(seed))
    spreads = {'L0_gnn_b1': (0.0, 0.683), 'L0_gnn_b2': (0.0, 0.279)}
    factors = {}
    for name, (base, spread) in spreads.items():
        noise = np.random.default_rng([zlib.crc32(name.encode()), seed]).standard_normal(out[name].shape)
        drawn = base * np.exp(spread * noise) if base else spread * noise
        out[name] = jnp.asarray(drawn.astype(out[name].dtype))
    for name, factor in factors.items():
        out[name] = (out[name] * factor).astype(out[name].dtype)
    return out
```

```python
import concourse.bass as bass
from concourse import mybir
from contextlib import ExitStack


def gnn_preln_kernel(nc, x, src, dst, edge_attr, w1, b1, w2, b2, out):
    f32, i32, u32 = mybir.dt.float32, mybir.dt.int32, mybir.dt.uint32
    ALU, ACT, AX = mybir.AluOpType, mybir.ActivationFunctionType, mybir.AxisListType

    N, D = x.shape
    E = src.shape[0]
    P = 128
    U = 4
    G = P * U
    NG = E // G
    ET = E - NG * G
    PT = ET // U
    assert PT * U == ET and PT > 0
    S = 5
    assert NG % S == 0
    NH = (NG + 1) // 2
    assert NH * 2 == NG + 1 and NH <= P
    WIN = 128
    NC = N // G
    NT = N - NC * G
    assert 0 < NT <= P and NC % 4 == 0
    LOADS = 4
    CL = NC // LOADS
    R = NC * U + 1
    ROW_LOADS = 2 + -(-G // ET)
    EPS = 1e-5

    def first(nth):
        return isinstance(nth, int) and nth == 1

    h_rows = nc.dram_tensor("h_rows", (N, D), f32).ap()

    x_chunks = x[0:NC * G, :].rearrange("(c p u) d -> p c (u d)", p=P, u=U)
    h_chunks = h_rows[0:NC * G, :].rearrange("(c p u) d -> c p (u d)", p=P, u=U)
    out_chunks = out[0:NC * G, :].rearrange("(c p u) d -> c p (u d)", p=P, u=U)
    edge_groups = edge_attr[0:NG * G, :].rearrange("(g p u) d -> g p (u d)", p=P, u=U)
    edge_rest = edge_attr[NG * G:E, :].rearrange("(p u) d -> p (u d)", u=U)

    with ExitStack() as ctx:
        def sb(name, shape, dt=f32):
            return ctx.enter_context(nc.sbuf_tensor(name, shape, dt))

        def sem(name):
            return ctx.enter_context(nc.semaphore(name))

        def sems(name, n):
            return [sem(f"{name}{i}") for i in range(n)]

        x_all = sb("x_all", [P, R * D])
        h_all = sb("h_all", [P, R * D])
        accT = sb("accT", [P, (NC + 1) * G])
        stats = sb("stats", [P, R, 6])
        mean2 = sb("mean2", [P, R])
        apart = sb("apart", [P, R])
        apart2 = sb("apart2", [P, R])
        varD = sb("varD", [P, R])
        std = sb("std", [P, R])
        rstd = sb("rstd", [P, R])
        shift = sb("shift", [P, R])
        eps = sb("eps", [P, 1])
        ident = sb("ident", [P, P])
        ones = sb("ones", [P, P])
        iota_sb = sb("iota_sb", [P, WIN])
        src_i = sb("src_i", [NH, 2, G], i32)
        dst_i = sb("dst_i", [NH, 2, G], i32)
        src_f = sb("src_f", [NH, 2, G])
        dst_f = sb("dst_f", [NH, 2, G])
        lo = sb("lo", [NH, 2])
        hi = sb("hi", [NH, 2])
        spread = sb("spread", [NH, 2])
        lo_diag = sb("lo_diag", [NH, 2, NH])
        spread_diag = sb("spread_diag", [NH, 2, NH])
        base_bc = sb("base_bc", [P, 2 * NH])
        base_i = sb("base_i", [1, 2 * NH], i32)
        spread_i = sb("spread_i", [1, 2 * NH], i32)
        more_i = sb("more_i", [1, 2 * NH], i32)
        src_all = sb("src_all", [P, 2 * NH * U])
        dst_rel = sb("dst_rel", [P, 2 * NH * U])
        idx = sb("idx", [P, S, U], u32)
        edges = sb("edges", [P, S, G])
        onehot = sb("onehot", [P, S, G])
        rel_more = sb("rel_more", [P, U])
        onehot_more = sb("onehot_more", [P, G])
        w1_sb = sb("w1_sb", [D, D])
        w2_sb = sb("w2_sb", [D, D])
        b1_sb = sb("b1_sb", [D, 1])
        b2_bc = sb("b2_bc", [P, D])
        biased = sb("biased", [P, 2, G])
        hidT = sb("hidT", [P, 2, G])
        y_sb = sb("y_sb", [P, 2, G])

        sum_ps = [ctx.enter_context(nc.psum_tensor(f"sum_ps{s}", [P, G], f32)) for s in range(S)]
        wide_ps = [ctx.enter_context(nc.psum_tensor(f"wide_ps{s}", [P, G], f32)) for s in range(2)]
        iota_ps = ctx.enter_context(nc.psum_tensor("iota_ps", [P, WIN], f32))
        src_ps, dst_ps, row_ps, more_ps = sum_ps[0:2], sum_ps[2:4], sum_ps[4], wide_ps[0]

        x_loaded = sems("x_loaded", LOADS)
        x_rest_loaded = sem("x_rest_loaded")
        src_loaded = sem("src_loaded")
        dst_loaded = sem("dst_loaded")
        weights_loaded = sem("weights_loaded")
        iota_ready = sem("iota_ready")
        iota_placed = sem("iota_placed")
        zeroed = sem("zeroed")
        ident_ready = sem("ident_ready")
        consts_ready = sem("consts_ready")
        stats_done = sem("stats_done")
        halves_met = sem("halves_met")
        squared = sem("squared")
        moments_ready = sem("moments_ready")
        std_ready = sem("std_ready")
        rstd_done = sem("rstd_done")
        norm_ready = sem("norm_ready")
        h_ready = sem("h_ready")
        h_stored = sem("h_stored")
        hT_ready = sem("hT_ready")
        acc_started = sem("acc_started")
        src_floats = sem("src_floats")
        dst_floats = sem("dst_floats")
        bounds_ready = sem("bounds_ready")
        spread_ready = sem("spread_ready")
        diags_ready = sem("diags_ready")
        src_turned = sem("src_turned")
        dst_turned = sem("dst_turned")
        rows_ready = sem("rows_ready")
        base_copied = sem("base_copied")
        src_all_ready = sem("src_all_ready")
        spread_copied = sem("spread_copied")
        tables_ready = sem("tables_ready")
        xb_ready = sem("xb_ready")

        slot_free = sems("slot_free", S)
        idx_ready = sems("idx_ready", S)
        edges_loaded = sems("edges_loaded", S)
        rows_gathered = sems("rows_gathered", S)
        onehot_ready = sems("onehot_ready", S)
        sum_ready = sems("sum_ready", S)
        more_onehot_ready = sem("more_onehot_ready")
        more_sum_ready = sem("more_sum_ready")
        acc_done = sem("acc_done")
        added = sem("added")
        gathers_begun = sem("gathers_begun")

        wide_ready = sems("wide_ready", 2)
        biased_ready = sems("biased_ready", 2)
        hid_ready = sems("hid_ready", 2)
        y_ps_ready = sems("y_ps_ready", 2)
        y_ready = sems("y_ready", 2)
        y_stored = sems("y_stored", 2)

        block = ctx.enter_context(nc.Block())

        @block.sync
        def _(sp):
            for q in range(LOADS):
                sp.dma_start(x_all[:, q * CL * G:(q + 1) * CL * G].rearrange("p (c w) -> p c w", c=CL),
                             x_chunks[:, q * CL:(q + 1) * CL, :]).then_inc(x_loaded[q], 16)
            sp.dma_start(x_all[0:NT, NC * G:NC * G + D], x[NC * G:N, :]).then_inc(x_rest_loaded, 16)
            with sp.Fori(0, NC) as c:
                sp.wait_ge(h_ready, c + 1)
                sp.dma_start(h_chunks[c], h_all[:, bass.ds(c * G, G)]).then_inc(h_stored, 16)
            sp.wait_ge(h_ready, NC + 1)
            sp.dma_start(h_rows[NC * G:N, :], h_all[0:NT, NC * G:NC * G + D]).then_inc(h_stored, 16)
            with sp.Fori(0, NG // S) as i:
                for s in range(S):
                    sp.wait_ge(slot_free[s], i + 1)
                    sp.dma_start(edges[:, s, :], edge_groups[i * S + s]).then_inc(edges_loaded[s], 16)
            sp.wait_ge(slot_free[0], NG // S + 1)
            sp.dma_start(edges[0:PT, 0, :], edge_rest).then_inc(edges_loaded[0], 16)
            with sp.Fori(0, NC // 2) as j:
                for s in range(2):
                    sp.wait_ge(y_ready[s], j + 1)
                    sp.dma_start(out_chunks[j * 2 + s], y_sb[:, s, :]).then_inc(y_stored[s], 16)
            sp.wait_ge(y_ready[0], NC // 2 + 1)
            sp.dma_start(out[NC * G:N, :], y_sb[0:NT, 0, 0:D]).then_inc(y_stored[0], 16)
            sp.wait_ge(y_stored[0], 16 * (NC // 2 + 1))
            sp.wait_ge(y_stored[1], 16 * (NC // 2))

        @block.gpsimd
        def _(pool):
            nc.gpsimd.iota(iota_sb[:], [[1, WIN]], base=0, channel_multiplier=0,
                           allow_small_or_imprecise_dtypes=True).then_inc(iota_ready, 1)
            nc.gpsimd.memset(ident[:], 0.0).then_inc(zeroed, 1)
            nc.gpsimd.memset(ones[:], 1.0)
            nc.gpsimd.memset(eps[:], EPS)
            nc.gpsimd.memset(accT[:, N:(NC + 1) * G], 0.0).then_inc(consts_ready, 1)
            pool.wait_ge(zeroed, 1)
            nc.gpsimd.affine_select(out=ident[:], in_=ident[:], compare_op=ALU.not_equal, fill=1.0, base=0,
                                    pattern=[[-1, P]], channel_multiplier=1).then_inc(ident_ready, 1)
            pool.wait_ge(h_stored, 16 * (NC + 1))
            with pool.Fori(0, NG // S) as i:
                for s in range(S):
                    pool.wait_ge(idx_ready[s], i + 1)
                    pool.sem_inc(gathers_begun, 1)
                    pool.wait_ge(edges_loaded[s], 16 * (i + 1))
                    pool.sem_inc(gathers_begun, 1)
                    for u in range(U):
                        pool.indirect_dma_start(
                            out=edges[:, s, u * D:(u + 1) * D], out_offset=None, compute_op=ALU.add, in_=h_rows[:, :],
                            in_offset=bass.IndirectOffsetOnAxis(ap=idx[:, s, u:u + 1], axis=0),
                        ).then_inc(rows_gathered[s], 16)
            pool.wait_ge(idx_ready[0], NG // S + 1)
            pool.wait_ge(edges_loaded[0], 16*(NG // S + 1))
            for u in range(U):
                pool.indirect_dma_start(
                    out=edges[0:PT, 0, u * D:(u + 1) * D], out_offset=None, compute_op=ALU.add, in_=h_rows[:, :],
                    in_offset=bass.IndirectOffsetOnAxis(ap=idx[0:PT, 0, u:u + 1], axis=0),
                ).then_inc(rows_gathered[0], 16)

        @block.scalar
        def _(act):
            def load_rows(values, tile, loaded):
                act.dma_start(tile[:, 0, :], values[0:NH * G].rearrange("(g e) -> g e", e=G)).then_inc(loaded, 16)
                act.dma_start(tile[0:NH - 1, 1, :],
                              values[NH * G:NG * G].rearrange("(g e) -> g e", e=G)).then_inc(loaded, 16)
                for at in range(0, G, ET):
                    n = min(ET, G - at)
                    act.dma_start(tile[NH - 1:NH, 1, at:at + n],
                                  values[NG * G:NG * G + n].rearrange("(a e) -> a e", a=1)).then_inc(loaded, 16)

            load_rows(src, src_i, src_loaded)
            load_rows(dst, dst_i, dst_loaded)
            act.dma_start(w1_sb[:], w1).then_inc(weights_loaded, 16)
            act.dma_start(w2_sb[:], w2).then_inc(weights_loaded, 16)
            act.dma_start(b1_sb[:], b1.rearrange("(d a) -> d a", a=1)).then_inc(weights_loaded, 16)
            act.dma_start(b2_bc[:], b2.rearrange("(a d) -> a d", a=1).to_broadcast([P, D])).then_inc(weights_loaded, 16)

            act.wait_ge(consts_ready, 1)

            def deviation(q, r0, r1, p1):
                act.wait_ge(moments_ready, q + 1)
                nc.scalar.activation(std[0:p1, r0:r1], varD[0:p1, r0:r1], ACT.Sqrt, scale=1.0 / D,
                                     bias=eps[0:p1, :]).then_inc(std_ready, 1)

            def normalise(q):
                act.wait_ge(norm_ready, q + 1)
                with act.Fori(q * CL, (q + 1) * CL) as c:
                    for u in range(U):
                        last = nc.scalar.activation(
                            h_all[:, bass.ds(c * G + u * D, D)], x_all[:, bass.ds(c * G + u * D, D)], ACT.Relu,
                            bias=shift[:, bass.ds(c * U + u, 1)], scale=rstd[:, bass.ds(c * U + u, 1)])
                    last.then_inc(h_ready, 1)

            deviation(0, 0, CL * U, P)
            for q in range(1, LOADS):
                deviation(q, q * CL * U, (q + 1) * CL * U, P)
                normalise(q - 1)
            deviation(LOADS, R - 1, R, NT)
            normalise(LOADS - 1)
            act.wait_ge(norm_ready, LOADS + 1)
            nc.scalar.activation(h_all[0:NT, NC * G:NC * G + D], x_all[0:NT, NC * G:NC * G + D], ACT.Relu,
                                 bias=shift[0:NT, R - 1:R], scale=rstd[0:NT, R - 1:R]).then_inc(h_ready, 1)

            def place_indices(g, s):
                nc.scalar.copy(idx[:, s, :], src_all[:, bass.ds(g * U, U)]).then_inc(idx_ready[s], 1)

            act.wait_ge(src_turned, 1)
            for half in range(2):
                last = nc.scalar.copy(
                    src_all[:, half * NH * U:(half + 1) * NH * U].rearrange("p (g u) -> p u g", u=U),
                    src_ps[half][:, 0:NH * U].rearrange("p (u g) -> p u g", u=U))
            last.then_inc(src_all_ready, 1)
            act.wait_ge(src_all_ready, 1)
            for s in range(S):
                act.wait_ge(slot_free[s], 1)
                place_indices(s, s)
            act.wait_ge(rows_ready, 1)
            nc.scalar.copy(base_bc[:], row_ps[:, 0:2 * NH])
            nc.scalar.copy(base_i[:], row_ps[0:1, 0:2 * NH]).then_inc(base_copied, 1)
            nc.scalar.copy(spread_i[:], more_ps[0:1, 0:2 * NH]).then_inc(spread_copied, 1)
            with act.Fori(0, NC // 2) as j:
                for b in range(2):
                    act.wait_ge(hT_ready, j * 2 + b + 1)
                    nc.scalar.activation(
                        accT[:, bass.ds((j * 2 + b) * G, G)].rearrange("d (p u) -> d u p", u=U),
                        wide_ps[b][:].rearrange("d (u p) -> d u p", u=U), ACT.Copy, scale=2.0,
                    ).then_inc(acc_started, 1)
            act.wait_ge(hT_ready, NC + 1)
            nc.scalar.activation(accT[:, NC * G:N], wide_ps[0][:, 0:NT], ACT.Copy,
                                 scale=2.0).then_inc(acc_started, 1)
            with act.Fori(1, NG // S) as i:
                for s in range(S):
                    act.wait_ge(slot_free[s], i + 1)
                    place_indices(i * S + s, s)
            act.wait_ge(slot_free[0], NG // S + 1)
            place_indices(NG, 0)

            act.wait_ge(weights_loaded, 64)

            def add_bias(s, nth, n):
                act.wait_ge(wide_ready[s], nth)
                if not first(nth):
                    act.wait_ge(hid_ready[s], nth - 1)
                nc.scalar.activation(biased[:, s, 0:n], wide_ps[s][:, 0:n], ACT.Identity,
                                     bias=b1_sb[:, 0:1]).then_inc(biased_ready[s], 1)

            add_bias(0, 1, G)
            add_bias(1, 1, G)
            with act.Fori(1, NC // 2) as j:
                for s in range(2):
                    add_bias(s, j + 1, G)
            add_bias(0, NC // 2 + 1, G)

        @block.vector
        def _(dve):
            for s in range(S):
                dve.sem_inc(slot_free[s], 1)
            dve.sem_inc(added, 1)
            dve.wait_ge(iota_ready, 1)
            nc.vector.tensor_copy(iota_ps[:], iota_sb[:]).then_inc(iota_placed, 1)

            def scale_of(q, r0, r1, p1):
                dve.wait_ge(std_ready, q + 1)
                nc.vector.reciprocal(rstd[0:p1, r0:r1], std[0:p1, r0:r1]).then_inc(rstd_done, 1)
                dve.wait_ge(rstd_done, q + 1)
                nc.vector.scalar_tensor_tensor(out=shift[0:p1, r0:r1], in0=mean2[0:p1, r0:r1], scalar=-0.5,
                                               in1=rstd[0:p1, r0:r1], op0=ALU.mult,
                                               op1=ALU.mult).then_inc(norm_ready, 1)

            def aggregate(chunks, r0, r1, p1):
                half = stats[0:p1, r0:r1, :]
                dve.wait_ge(stats_done, chunks)
                nc.vector.tensor_tensor(mean2[0:p1, r0:r1], half[:, :, 1], half[:, :, 4], ALU.add)
                nc.vector.tensor_tensor(apart[0:p1, r0:r1], half[:, :, 1], half[:, :, 4], ALU.subtract)
                nc.vector.tensor_tensor(varD[0:p1, r0:r1], half[:, :, 2], half[:, :, 5], ALU.add).then_inc(halves_met, 1)
                met[0] += 1
                dve.wait_ge(halves_met, met[0])
                nc.vector.scalar_tensor_tensor(out=apart2[0:p1, r0:r1], in0=apart[0:p1, r0:r1], scalar=D / 4.0,
                                               in1=apart[0:p1, r0:r1], op0=ALU.mult, op1=ALU.mult).then_inc(squared, 1)
                dve.wait_ge(squared, met[0])
                nc.vector.tensor_tensor(varD[0:p1, r0:r1], varD[0:p1, r0:r1], apart2[0:p1, r0:r1],
                                        ALU.add).then_inc(moments_ready, 1)

            met = [0]
            for q in range(LOADS):
                dve.wait_ge(x_loaded[q], 16)
                with dve.Fori(q * CL, (q + 1) * CL) as c:
                    for u in range(U):
                        last = nc.vector.bn_stats(stats[:, bass.ds(c * U + u, 1), :].rearrange("p a k -> p (a k)"),
                                                  x_all[:, bass.ds(c * G + u * D, D)])
                    last.then_inc(stats_done, 1)
                aggregate((q + 1) * CL, q * CL * U, (q + 1) * CL * U, P)
                if q:
                    scale_of(q - 1, (q - 1) * CL * U, q * CL * U, P)
            dve.wait_ge(x_rest_loaded, 16)
            nc.vector.bn_stats(stats[0:NT, R - 1, :], x_all[0:NT, NC * G:NC * G + D]).then_inc(stats_done, 1)
            aggregate(NC + 1, R - 1, R, NT)
            scale_of(LOADS - 1, (LOADS - 1) * CL * U, LOADS * CL * U, P)
            scale_of(LOADS, R - 1, R, NT)

            dve.wait_ge(src_loaded, 16 * ROW_LOADS)
            nc.vector.tensor_copy(src_f[:], src_i[:]).then_inc(src_floats, 1)

            dve.wait_ge(dst_loaded, 16 * ROW_LOADS)
            nc.vector.tensor_copy(dst_f[:], dst_i[:]).then_inc(dst_floats, 1)
            dve.wait_ge(dst_floats, 1)
            nc.vector.tensor_reduce(lo[:], dst_f[:], AX.X, ALU.min)
            nc.vector.tensor_reduce(hi[:], dst_f[:], AX.X, ALU.max).then_inc(bounds_ready, 1)
            dve.wait_ge(bounds_ready, 1)
            nc.vector.tensor_tensor(spread[:], hi[:], lo[:], ALU.subtract).then_inc(spread_ready, 1)
            dve.wait_ge(ident_ready, 1)
            dve.wait_ge(spread_ready, 1)
            for half in range(2):
                nc.vector.tensor_scalar(lo_diag[:, half, :], ident[0:NH, 0:NH], lo[:, half:half + 1], None, ALU.mult)
                last = nc.vector.tensor_scalar(spread_diag[:, half, :], ident[0:NH, 0:NH],
                                               spread[:, half:half + 1], None, ALU.mult)
            last.then_inc(diags_ready, 1)
            dve.wait_ge(base_copied, 1)
            dve.wait_ge(dst_turned, 1)
            for half in range(2):
                nc.vector.tensor_tensor(
                    dst_rel[:, half * NH * U:(half + 1) * NH * U].rearrange("p (g u) -> p u g", u=U),
                    dst_ps[half][:, 0:NH * U].rearrange("p (u g) -> p u g", u=U),
                    base_bc[:, half * NH:(half + 1) * NH].unsqueeze(1).to_broadcast([P, U, NH]), ALU.subtract)
            dve.wait_ge(spread_copied, 1)
            nc.vector.tensor_scalar(more_i[:], spread_i[:], WIN.bit_length() - 1, None,
                                    ALU.arith_shift_right).then_inc(tables_ready, 1)
            dve.wait_ge(tables_ready, 1)
            dve.wait_ge(iota_placed, 1)

            def build_onehot(g, s):
                for u in range(U):
                    last = nc.vector.tensor_scalar(onehot[:, s, u * WIN:(u + 1) * WIN], iota_ps[:],
                                                   dst_rel[:, bass.ds(g * U + u, 1)], None, ALU.is_equal)
                last.then_inc(onehot_ready[s], 1)

            dve.wait_ge(weights_loaded, 64)
            dve.wait_ge(h_ready, NC + 1)
            nc.vector.tensor_tensor(x_all[:, 0:NC * G].rearrange("p (r d) -> p r d", d=D),
                                    x_all[:, 0:NC * G].rearrange("p (r d) -> p r d", d=D),
                                    b2_bc[:].unsqueeze(1).to_broadcast([P, NC * U, D]), ALU.add)
            nc.vector.tensor_tensor(x_all[0:NT, NC * G:NC * G + D], x_all[0:NT, NC * G:NC * G + D],
                                    b2_bc[0:NT, :], ALU.add).then_inc(xb_ready, 1)

            more_count = dve.alloc_register("dve_more_count")
            dve.reg_mov(more_count, 0)

            def add_group(g, s, nth):
                base = dve.value_load(base_i[0:1, bass.ds(g, 1)], min_val=0, max_val=N - 1)
                more = dve.value_load(more_i[0:1, bass.ds(g, 1)], min_val=0, max_val=(N - 1) // WIN)
                dve.wait_ge(sum_ready[s], nth)
                dve.wait_ge(added, g + 1)
                nc.vector.tensor_tensor(accT[:, bass.ds(base, WIN)], accT[:, bass.ds(base, WIN)],
                                        sum_ps[s][:, 0:WIN], ALU.add).then_inc(added, 1)
                with dve.If(more > 0):
                    nc.vector.tensor_copy(rel_more[:], dst_rel[:, bass.ds(g * U, U)])
                    with dve.Fori(0, more) as k:
                        dve.drain()
                        nc.vector.tensor_scalar(rel_more[:], rel_more[:], -float(WIN), None, ALU.add)
                        dve.drain()
                        for u in range(U):
                            last = nc.vector.tensor_scalar(onehot_more[:, u * WIN:(u + 1) * WIN], iota_ps[:],
                                                           rel_more[:, u:u + 1], None, ALU.is_equal)
                        last.then_inc(more_onehot_ready, 1)
                        dve.reg_add(more_count, more_count, 1)
                        at = nc.s_assert_within(dve.snap(base + k * WIN + WIN), 0, N - 1)
                        dve.wait_ge(more_sum_ready, dve.snap(more_count))
                        nc.vector.tensor_tensor(accT[:, bass.ds(at, WIN)], accT[:, bass.ds(at, WIN)],
                                                wide_ps[1][:, 0:WIN], ALU.add)
                    dve.drain()
                dve.sem_inc(slot_free[s], 1)

            build_onehot(0, 0)
            dve.wait_ge(acc_started, NC + 1)
            with dve.Fori(0, NG // S) as i:
                for s in range(S):
                    build_onehot(i * S + s + 1, (s + 1) % S)
                    add_group(i * S + s, s, i + 1)
            add_group(NG, 0, NG // S + 1)
            dve.drain().then_inc(acc_done, 1)

            def leaky_relu(s, nth, n):
                dve.wait_ge(biased_ready[s], nth)
                if not first(nth):
                    dve.wait_ge(y_ps_ready[s], nth - 1)
                nc.vector.scalar_tensor_tensor(out=hidT[:, s, 0:n], in0=biased[:, s, 0:n], scalar=0.01,
                                               in1=biased[:, s, 0:n], op0=ALU.mult,
                                               op1=ALU.max).then_inc(hid_ready[s], 1)

            dve.wait_ge(xb_ready, 1)

            def finish(c, s, nth, n, w):
                dve.wait_ge(y_ps_ready[s], nth)
                if not first(nth):
                    dve.wait_ge(y_stored[s], 16 * (nth - 1))
                nc.vector.tensor_tensor(y_sb[0:n, s, 0:w], sum_ps[s][0:n, 0:w],
                                        x_all[0:n, bass.ds(c * G, w)], ALU.add).then_inc(y_ready[s], 1)

            def finish_pair(j):
                leaky_relu(1, j + 1, G)
                finish(j * 2, 0, j + 1, P, G)
                leaky_relu(0, j + 2, G)
                finish(j * 2 + 1, 1, j + 1, P, G)

            leaky_relu(0, 1, G)
            finish_pair(0)
            with dve.Fori(1, NC // 2) as j:
                finish_pair(j)
            finish(NC, 0, NC // 2 + 1, NT, D)

        @block.tensor
        def _(pe):
            pe.wait_ge(ident_ready, 1)

            def turn_rows(table, halves):
                for half in range(2):
                    for u in range(U):
                        last = nc.tensor.transpose(halves[half][:, u * NH:(u + 1) * NH], table[:, half, u:G:U],
                                                   ident[0:NH, 0:NH])
                return last

            pe.wait_ge(src_floats, 1)
            turn_rows(src_f, src_ps).then_inc(src_turned, 1)
            pe.wait_ge(dst_floats, 1)
            turn_rows(dst_f, dst_ps).then_inc(dst_turned, 1)
            pe.wait_ge(consts_ready, 1)
            pe.wait_ge(diags_ready, 1)
            nc.tensor.matmul(row_ps[:, 0:2 * NH], ones[0:NH, :], lo_diag[:].rearrange("k a g -> k (a g)"),
                             start=True, stop=True)
            nc.tensor.matmul(more_ps[:, 0:2 * NH], ones[0:NH, :], spread_diag[:].rearrange("k a g -> k (a g)"),
                             start=True, stop=True).then_inc(rows_ready, 1)

            pe.wait_ge(spread_copied, 1)
            for c in range(NC):
                pe.wait_ge(h_ready, c + 1)
                if c >= 2:
                    pe.wait_ge(acc_started, c - 1)
                for u in range(U):
                    last = nc.tensor.transpose(wide_ps[c % 2][:, u * P:(u + 1) * P],
                                               h_all[:, c * G + u * D:c * G + (u + 1) * D], ident[:])
                last.then_inc(hT_ready, 1)
            pe.wait_ge(h_ready, NC + 1)
            pe.wait_ge(acc_started, NC - 1)
            nc.tensor.transpose(wide_ps[0][:, 0:NT], h_all[0:NT, NC * G:NC * G + D],
                                ident[0:NT, 0:NT]).then_inc(hT_ready, 1)
            pe.wait_ge(src_all_ready, 1)
            pe.wait_ge(base_copied, 1)
            pe.wait_ge(acc_started, NC)

            pe.wait_ge(tables_ready, 1)
            more_count = pe.alloc_register("pe_more_count")
            pe.reg_mov(more_count, 0)

            def sum_slot(into, hot, s, p1):
                for u in range(U):
                    last = nc.tensor.matmul(into[:, 0:WIN], edges[0:p1, s, u * D:(u + 1) * D],
                                            hot[0:p1, u * WIN:(u + 1) * WIN],
                                            start=(u == 0), stop=(u == U - 1))
                return last

            def sum_group(g, s, nth, p1):
                more = pe.value_load(more_i[0:1, bass.ds(g, 1)], min_val=0, max_val=(N - 1) // WIN)
                pe.wait_ge(onehot_ready[s], nth)
                pe.wait_ge(rows_gathered[s], 16 * U * nth)
                sum_slot(sum_ps[s], onehot[:, s, :], s, p1).then_inc(sum_ready[s], 1)
                with pe.If(more > 0):
                    with pe.Fori(0, more):
                        pe.reg_add(more_count, more_count, 1)
                        pe.wait_ge(more_onehot_ready, pe.snap(more_count))
                        sum_slot(wide_ps[1], onehot_more[:], s, p1).then_inc(more_sum_ready, 1)

            with pe.Fori(0, NG // S) as i:
                for s in range(S):
                    sum_group(i * S + s, s, i + 1, P)
            sum_group(NG, 0, NG // S + 1, PT)

            pe.wait_ge(acc_done, 1)
            pe.wait_ge(weights_loaded, 64)

            def first_layer(c, s, nth):
                if not first(nth):
                    pe.wait_ge(biased_ready[s], nth - 1)
                nc.tensor.matmul(wide_ps[s][:], w1_sb[:], accT[:, bass.ds(c * G, G)],
                                 start=True, stop=True).then_inc(wide_ready[s], 1)

            def second_layer(s, nth, tiles):
                pe.wait_ge(hid_ready[s], nth)
                if not first(nth):
                    pe.wait_ge(y_ready[s], nth - 1)
                for at, (n, nodes) in enumerate(tiles):
                    last = nc.tensor.matmul(sum_ps[s][0:n, at * D:(at + 1) * D], nodes, w2_sb[:],
                                            start=True, stop=True)
                last.then_inc(y_ps_ready[s], 1)

            def tiles_of(s):
                return [(P, hidT[:, s, u:G:U]) for u in range(U)]

            def layer_pair(j):
                first_layer(j * 2 + 1, 1, j + 1)
                second_layer(0, j + 1, tiles_of(0))
                first_layer(j * 2 + 2, 0, j + 2)
                second_layer(1, j + 1, tiles_of(1))

            first_layer(0, 0, 1)
            layer_pair(0)
            with pe.Fori(1, NC // 2) as j:
                layer_pair(j)
            second_layer(0, NC // 2 + 1, [(NT, hidT[:, 0, 0:NT])])


_INS = ["x", "src", "dst", "edge_attr_128", "L0_gnn_W1", "L0_gnn_b1", "L0_gnn_W2", "L0_gnn_b2"]


def kernel(**inputs):
    import numpy as _np
    import concourse.bacc as _bacc
    from concourse import mybir as _mybir
    from concourse.bass_utils import run_bass_kernel_spmd as _run

    nc = _bacc.Bacc("TRN2", target_bir_lowering=False, num_devices=1)
    arrays, args = {}, []
    for name in _INS:
        a = _np.ascontiguousarray(inputs[name])
        arrays[f"in_{name}"] = a
        args.append(nc.dram_tensor(f"in_{name}", a.shape, _mybir.dt.from_np(a.dtype), kind="ExternalInput").ap())
    shape = inputs["x"].shape
    args.append(nc.dram_tensor("out_0", shape, _mybir.dt.float32, kind="ExternalOutput").ap())
    gnn_preln_kernel(nc, *args)
    r = _run(nc, [arrays], core_ids=[0])
    return r.results[0]["out_0"]
```

```python
import concourse.bass as bass
from concourse import mybir
from contextlib import ExitStack


def gnn_preln_kernel(nc, x, src, dst, edge_attr, w1, b1, w2, b2, out):
    f32, i32, u32, bf16 = mybir.dt.float32, mybir.dt.int32, mybir.dt.uint32, mybir.dt.bfloat16
    ALU, ACT, AX = mybir.AluOpType, mybir.ActivationFunctionType, mybir.AxisListType

    N, D = x.shape
    E = src.shape[0]
    P = 128
    U = 4
    G = P * U
    NG = E // G
    ET = E - NG * G
    PT = ET // U
    assert PT * U == ET and PT > 0
    S = 8
    HS = 4
    SP = S // HS
    RS = SP + 1
    ORDER = [x for k in range(HS) for x in [S + k, *range(k * SP, (k + 1) * SP)]]
    Q = len(ORDER)
    TILES = [(0, 1), (2, 3), ()]
    assert len(TILES) == RS and Q % 2 == 0
    HR = NG // Q
    ADDS = Q + HS
    W0 = RS
    HG = HR * HS
    HT = HG * U
    LEFT = NG - HR * Q
    assert HR >= 3 and LEFT + 1 <= S and HS <= LEFT + 1 and W0 + HS <= Q
    NH = (NG + 1) // 2
    assert NH * 2 == NG + 1 and NH <= P
    WIN = 128
    NC = N // G
    NT = N - NC * G
    assert 0 < NT <= P and NC % 4 == 0
    LOADS = 4
    CL = NC // LOADS
    R = NC * U + 1
    ROW_LOADS = 2 + -(-G // ET)
    HI = R
    HW = 31
    ZW = HI * HW
    DIV = -(-65536 // HW)
    MORE_MAX = (N - 1) * DIV // 65536
    assert ZW <= 3 * 512 and HS * HW <= 512 and HG <= NH and (N - 1) * DIV < 1 << 24
    EPS = 1e-5

    def first(nth):
        return isinstance(nth, int) and nth == 1

    def group_of(it, slot):
        return HG + it * S + slot if slot < S else it * HS + slot - S

    h_rows = nc.dram_tensor("h_rows", (N, D), f32).ap()

    x_chunks = x[0:NC * G, :].rearrange("(c p u) d -> p c (u d)", p=P, u=U)
    h_chunks = h_rows[0:NC * G, :].rearrange("(c p u) d -> c p (u d)", p=P, u=U)
    out_chunks = out[0:NC * G, :].rearrange("(c p u) d -> c p (u d)", p=P, u=U)
    edge_groups = edge_attr[0:NG * G, :].rearrange("(g p u) d -> g p (u d)", p=P, u=U)
    edge_rest = edge_attr[NG * G:E, :].rearrange("(p u) d -> p (u d)", u=U)

    with ExitStack() as ctx:
        def sb(name, shape, dt=f32):
            return ctx.enter_context(nc.sbuf_tensor(name, shape, dt))

        def sem(name):
            return ctx.enter_context(nc.semaphore(name))

        def sems(name, n):
            return [sem(f"{name}{i}") for i in range(n)]

        x_all = sb("x_all", [P, R * D])
        h_all = sb("h_all", [P, R * D])
        accT = sb("accT", [P, (NC + 1) * G])
        stats = sb("stats", [P, R, 6])
        mean2 = sb("mean2", [P, R])
        apart = sb("apart", [P, R])
        apart2 = sb("apart2", [P, R])
        varD = sb("varD", [P, R])
        std = sb("std", [P, R])
        rstd = sb("rstd", [P, R])
        shift = sb("shift", [P, R])
        eps = sb("eps", [P, 1])
        ident = sb("ident", [P, P])
        ones = sb("ones", [P, P])
        iota_sb = sb("iota_sb", [P, WIN])
        src_i_full = sb("src_i", [P, 2, G], i32)
        src_i = src_i_full[0:NH]
        dst_i = sb("dst_i", [NH, 2, G], i32)
        src_f = sb("src_f", [NH, 2, G])
        dst_f = sb("dst_f", [NH, 2, G])
        lo = sb("lo", [NH, 2])
        hi = sb("hi", [NH, 2])
        spread = sb("spread", [NH, 2])
        lo_diag = sb("lo_diag", [NH, 2, NH])
        spread_diag = sb("spread_diag", [NH, 2, NH])
        base_bc = sb("base_bc", [P, 2 * NH])
        base_i = sb("base_i", [1, 2 * NH], i32)
        spread_i = sb("spread_i", [1, 2 * NH], i32)
        more_i = sb("more_i", [1, 2 * NH], i32)
        src_all = sb("src_all", [P, 2 * NH * U])
        dst_rel = sb("dst_rel", [P, 2 * NH * U])
        idx = sb("idx", [P, S, U], u32)
        edges = sb("edges", [P, S + HS, G])
        onehot = sb("onehot", [P, 2, G])
        h_part = [sb(f"h_part{k}", [P, HI * D], bf16) for k in range(3)]
        counts = sb("counts", [P, HI, HS, HW], mybir.dt.float16)
        iota_z = sb("iota_z", [P, ZW], mybir.dt.int16)
        iota_lo = sb("iota_lo", [P, P], bf16)
        pair_hot = sb("pair_hot", [P, U, ZW], bf16)
        low_hot = sb("low_hot", [P, U, P], bf16)
        low = sb("low", [P, HT])
        high_key = sb("high_key", [P, HT])
        pair_key = sb("pair_key", [P, HT])
        widest = sb("widest", [1, 2, HR])
        head_spread = sb("head_spread", [1, HG + HG // HS * S])
        head_scaled_i = sb("head_scaled_i", [1, HG + HR], i32)
        head_more_i = sb("head_more_i", [1, HG + HR], i32)
        dst_more = sb("dst_more", [P, U])
        in_more = sb("in_more", [P, U])
        key_more = sb("key_more", [P, U])
        rel_more = sb("rel_more", [P, U])
        onehot_more = sb("onehot_more", [P, G])
        spare_i = src_i_full[:].rearrange("p a (b t) -> p (a b) t", t=HT)
        src_h, part_i = spare_i[:, 0, :], spare_i[:, 1:4, :]
        spare = onehot[:].rearrange("p a (b t) -> p (a b) t", t=HT)
        parts, in_tail = spare[:, 0:3, :], spare[:, 3, :]
        tail_diff = onehot_more[:].rearrange("p (b t) -> p b t", t=HT)
        w1_sb = sb("w1_sb", [D, D])
        w2_sb = sb("w2_sb", [D, D])
        b1_sb = sb("b1_sb", [D, 1])
        b2_bc = sb("b2_bc", [P, D])
        biased, hidT, y_sb = edges[:, 4:6, :], edges[:, 6:8, :], edges[:, 8:10, :]

        def bank(name, width=512):
            return ctx.enter_context(nc.psum_tensor(name, [P, width], f32))

        a_ps = bank("a_ps", 3 * 512)
        sum_ps = [bank("sum_ps0"), bank("sum_ps1")]
        win_ps = bank("win_ps")
        extra_ps = bank("extra_ps")
        iota_ps = bank("iota_ps")
        a_banks = [a_ps[:, k * 512:(k + 1) * 512] for k in range(3)]
        src_ps, dst_ps, row_ps = a_banks[0:2], sum_ps, a_banks[2]
        turn_ps = [win_ps, extra_ps]
        wide_ps = a_banks[0:2]

        x_loaded = sems("x_loaded", LOADS)
        x_rest_loaded = sem("x_rest_loaded")
        src_loaded = sem("src_loaded")
        dst_loaded = sem("dst_loaded")
        weights_loaded = sem("weights_loaded")
        iota_ready = sem("iota_ready")
        iota_placed = sem("iota_placed")
        zeroed = sem("zeroed")
        ident_ready = sem("ident_ready")
        consts_ready = sem("consts_ready")
        h_tail_zeroed = sem("h_tail_zeroed")
        head_consts_ready = sem("head_consts_ready")
        stats_done = sem("stats_done")
        halves_met = sem("halves_met")
        squared = sem("squared")
        moments_ready = sem("moments_ready")
        std_ready = sem("std_ready")
        rstd_done = sem("rstd_done")
        norm_ready = sem("norm_ready")
        h_ready = sem("h_ready")
        h_stored = sem("h_stored")
        hT_ready = sem("hT_ready")
        acc_started = sem("acc_started")
        src_floats = sem("src_floats")
        dst_floats = sem("dst_floats")
        bounds_ready = sem("bounds_ready")
        spread_ready = sem("spread_ready")
        diags_ready = sem("diags_ready")
        src_turned = sem("src_turned")
        dst_turned = sem("dst_turned")
        rows_ready = sem("rows_ready")
        base_copied = sem("base_copied")
        src_all_ready = sem("src_all_ready")
        spread_copied = sem("spread_copied")
        tables_ready = sem("tables_ready")
        xb_ready = sem("xb_ready")

        slot_free = sems("slot_free", S + HS)
        idx_ready = sems("idx_ready", S)
        edges_loaded = sems("edges_loaded", S + HS)
        rows_gathered = sems("rows_gathered", S)
        onehot_ready = sem("onehot_ready")
        sum_ready = sem("sum_ready")
        h_split = sem("h_split")
        pair_ready = sem("pair_ready")
        counted = sem("counted")
        counts_copied = sem("counts_copied")
        window_ready = sem("window_ready")
        more_pair_ready = sem("more_pair_ready")
        more_counted = sem("more_counted")
        more_copied = sem("more_copied")
        more_window_ready = sem("more_window_ready")
        more_onehot_ready = sem("more_onehot_ready")
        more_sum_ready = sem("more_sum_ready")
        acc_done = sem("acc_done")
        added = sem("added")
        gathers_begun = sem("gathers_begun")

        wide_ready = sems("wide_ready", 2)
        biased_ready = sems("biased_ready", 2)
        hid_ready = sems("hid_ready", 2)
        y_ps_ready = sems("y_ps_ready", 2)
        y_ready = sems("y_ready", 2)
        y_stored = sems("y_stored", 2)

        block = ctx.enter_context(nc.Block())

        @block.sync
        def _(sp):
            for q in range(LOADS):
                sp.dma_start(x_all[:, q * CL * G:(q + 1) * CL * G].rearrange("p (c w) -> p c w", c=CL),
                             x_chunks[:, q * CL:(q + 1) * CL, :]).then_inc(x_loaded[q], 16)
            sp.dma_start(x_all[0:NT, NC * G:NC * G + D], x[NC * G:N, :]).then_inc(x_rest_loaded, 16)
            with sp.Fori(0, NC) as c:
                sp.wait_ge(h_ready, c + 1)
                sp.dma_start(h_chunks[c], h_all[:, bass.ds(c * G, G)]).then_inc(h_stored, 16)
            sp.wait_ge(h_ready, NC + 1)
            sp.dma_start(h_rows[NC * G:N, :], h_all[0:NT, NC * G:NC * G + D]).then_inc(h_stored, 16)
            def load_edges(it, slot):
                sp.wait_ge(slot_free[slot], it + 1)
                sp.dma_start(edges[:, slot, :], edge_groups[group_of(it, slot)]).then_inc(edges_loaded[slot], 16)

            with sp.Fori(0, HR) as it:
                for slot in ORDER:
                    load_edges(it, slot)
            for slot in range(LEFT):
                load_edges(HR, slot)
            sp.wait_ge(slot_free[LEFT], HR + 1)
            sp.dma_start(edges[0:PT, LEFT, :], edge_rest).then_inc(edges_loaded[LEFT], 16)
            with sp.Fori(0, NC // 2) as j:
                for s in range(2):
                    sp.wait_ge(y_ready[s], j + 1)
                    sp.dma_start(out_chunks[j * 2 + s], y_sb[:, s, :]).then_inc(y_stored[s], 16)
            sp.wait_ge(y_ready[0], NC // 2 + 1)
            sp.dma_start(out[NC * G:N, :], y_sb[0:NT, 0, 0:D]).then_inc(y_stored[0], 16)
            sp.wait_ge(y_stored[0], 16 * (NC // 2 + 1))
            sp.wait_ge(y_stored[1], 16 * (NC // 2))

        @block.gpsimd
        def _(pool):
            nc.gpsimd.iota(iota_sb[:], [[1, WIN]], base=0, channel_multiplier=0,
                           allow_small_or_imprecise_dtypes=True).then_inc(iota_ready, 1)
            nc.gpsimd.memset(ident[:], 0.0).then_inc(zeroed, 1)
            nc.gpsimd.memset(ones[:], 1.0)
            nc.gpsimd.memset(eps[:], EPS)
            nc.gpsimd.memset(accT[:, N:(NC + 1) * G], 0.0).then_inc(consts_ready, 1)
            nc.gpsimd.iota(iota_z[:], [[1, ZW]], base=0, channel_multiplier=0, allow_small_or_imprecise_dtypes=True)
            nc.gpsimd.iota(iota_lo[:], [[1, P]], base=0, channel_multiplier=0,
                           allow_small_or_imprecise_dtypes=True).then_inc(head_consts_ready, 1)
            nc.gpsimd.memset(h_all[:, NC * G:NC * G + D], 0.0).then_inc(h_tail_zeroed, 1)
            pool.wait_ge(zeroed, 1)
            nc.gpsimd.affine_select(out=ident[:], in_=ident[:], compare_op=ALU.not_equal, fill=1.0, base=0,
                                    pattern=[[-1, P]], channel_multiplier=1).then_inc(ident_ready, 1)
            pool.wait_ge(h_stored, 16 * (NC + 1))
            def gather(slot, nth, p1):
                pool.wait_ge(idx_ready[slot], nth)
                pool.sem_inc(gathers_begun, 1)
                pool.wait_ge(edges_loaded[slot], 16 * nth)
                pool.sem_inc(gathers_begun, 1)
                for u in range(U):
                    pool.indirect_dma_start(
                        out=edges[0:p1, slot, u * D:(u + 1) * D], out_offset=None, in_=h_rows[:, :],
                        in_offset=bass.IndirectOffsetOnAxis(ap=idx[0:p1, slot, u:u + 1], axis=0),
                        compute_op=ALU.add).then_inc(rows_gathered[slot], 16)

            with pool.Fori(0, HR) as it:
                for slot in range(S):
                    gather(slot, it + 1, P)
            for slot in range(LEFT):
                gather(slot, HR + 1, P)
            gather(LEFT, HR + 1, PT)

            pool.wait_ge(weights_loaded, 64)
            pool.wait_ge(h_ready, NC + 1)
            with pool.Fori(0, NC) as c:
                nc.gpsimd.tensor_tensor(x_all[:, bass.ds(c * G, G)].rearrange("p (u d) -> p u d", u=U),
                                        x_all[:, bass.ds(c * G, G)].rearrange("p (u d) -> p u d", u=U),
                                        b2_bc[:].unsqueeze(1).to_broadcast([P, U, D]), ALU.add).then_inc(xb_ready, 1)
            nc.gpsimd.tensor_tensor(x_all[0:NT, NC * G:NC * G + D], x_all[0:NT, NC * G:NC * G + D],
                                    b2_bc[0:NT, :], ALU.add).then_inc(xb_ready, 1)

        @block.scalar
        def _(act):
            def load_rows(values, tile, loaded):
                act.dma_start(tile[:, 0, :], values[0:NH * G].rearrange("(g e) -> g e", e=G)).then_inc(loaded, 16)
                act.dma_start(tile[0:NH - 1, 1, :],
                              values[NH * G:NG * G].rearrange("(g e) -> g e", e=G)).then_inc(loaded, 16)
                for at in range(0, G, ET):
                    n = min(ET, G - at)
                    act.dma_start(tile[NH - 1:NH, 1, at:at + n],
                                  values[NG * G:NG * G + n].rearrange("(a e) -> a e", a=1)).then_inc(loaded, 16)

            load_rows(src, src_i, src_loaded)
            load_rows(dst, dst_i, dst_loaded)
            act.dma_start(w1_sb[:], w1).then_inc(weights_loaded, 16)
            act.dma_start(w2_sb[:], w2).then_inc(weights_loaded, 16)
            act.dma_start(b1_sb[:], b1.rearrange("(d a) -> d a", a=1)).then_inc(weights_loaded, 16)
            act.dma_start(b2_bc[:], b2.rearrange("(a d) -> a d", a=1).to_broadcast([P, D])).then_inc(weights_loaded, 16)

            act.wait_ge(consts_ready, 1)

            def deviation(q, r0, r1, p1):
                act.wait_ge(moments_ready, q + 1)
                nc.scalar.activation(std[0:p1, r0:r1], varD[0:p1, r0:r1], ACT.Sqrt, scale=1.0 / D,
                                     bias=eps[0:p1, :]).then_inc(std_ready, 1)

            def normalise(q):
                act.wait_ge(norm_ready, q + 1)
                with act.Fori(q * CL, (q + 1) * CL) as c:
                    for u in range(U):
                        last = nc.scalar.activation(
                            h_all[:, bass.ds(c * G + u * D, D)], x_all[:, bass.ds(c * G + u * D, D)], ACT.Relu,
                            bias=shift[:, bass.ds(c * U + u, 1)], scale=rstd[:, bass.ds(c * U + u, 1)])
                    last.then_inc(h_ready, 1)

            deviation(0, 0, CL * U, P)
            for q in range(1, LOADS):
                deviation(q, q * CL * U, (q + 1) * CL * U, P)
                normalise(q - 1)
            deviation(LOADS, R - 1, R, NT)
            normalise(LOADS - 1)
            act.wait_ge(norm_ready, LOADS + 1)
            act.wait_ge(h_tail_zeroed, 1)
            nc.scalar.activation(h_all[0:NT, NC * G:NC * G + D], x_all[0:NT, NC * G:NC * G + D], ACT.Relu,
                                 bias=shift[0:NT, R - 1:R], scale=rstd[0:NT, R - 1:R]).then_inc(h_ready, 1)

            def place_indices(it, slots):
                for slot in slots:
                    act.wait_ge(slot_free[slot], it + 1)
                    nc.scalar.copy(idx[:, slot, :],
                                   src_all[:, bass.ds(group_of(it, slot) * U, U)]).then_inc(idx_ready[slot], 1)

            act.wait_ge(src_turned, 1)
            for half in range(2):
                last = nc.scalar.copy(
                    src_all[:, half * NH * U:(half + 1) * NH * U].rearrange("p (g u) -> p u g", u=U),
                    src_ps[half][:, 0:NH * U].rearrange("p (u g) -> p u g", u=U))
            last.then_inc(src_all_ready, 1)
            act.wait_ge(src_all_ready, 1)
            place_indices(0, range(S))
            act.wait_ge(rows_ready, 1)
            nc.scalar.copy(base_bc[:], row_ps[:, 0:2 * NH])
            nc.scalar.copy(base_i[:], row_ps[0:1, 0:2 * NH])
            nc.scalar.copy(spread_i[:], row_ps[0:1, 2 * NH:4 * NH]).then_inc(base_copied, 1)
            nc.scalar.copy(head_spread[:], row_ps[0:1, 2 * NH:2 * NH + HR * Q]).then_inc(spread_copied, 1)
            with act.Fori(0, NC // 2) as j:
                for b in range(2):
                    act.wait_ge(hT_ready, j * 2 + b + 1)
                    nc.scalar.activation(
                        accT[:, bass.ds((j * 2 + b) * G, G)].rearrange("d (p u) -> d u p", u=U),
                        turn_ps[b][:].rearrange("d (u p) -> d u p", u=U), ACT.Copy, scale=2.0,
                    ).then_inc(acc_started, 1)
            act.wait_ge(hT_ready, NC + 1)
            nc.scalar.activation(accT[:, NC * G:N], turn_ps[0][:, 0:NT], ACT.Copy,
                                 scale=2.0).then_inc(acc_started, 1)

            nc.scalar.copy(h_part[0][:], h_all[:]).then_inc(h_split, 1)

            more_count = act.alloc_register("act_more_count")
            act.reg_mov(more_count, 0)
            act.wait_ge(tables_ready, 1)

            def copy_counts(k):
                return nc.scalar.copy(counts[:, :, k, :], a_ps[:, 0:ZW].rearrange("p (t n) -> p t n", n=HW))

            def further_windows(it):
                more_of_round = act.value_load(head_more_i[0:1, bass.ds(HG + it, 1)], min_val=0, max_val=MORE_MAX)
                with act.If(more_of_round > 0):
                    with act.Fori(0, HS) as k:
                        more = act.value_load(head_more_i[0:1, bass.ds(it * HS + k, 1)], min_val=0, max_val=MORE_MAX)
                        with act.If(more > 0):
                            with act.Fori(0, more):
                                act.reg_add(more_count, more_count, 1)
                                act.wait_ge(more_counted, act.snap(more_count))
                                copy_counts(0).then_inc(more_copied, 1)

            def head_round(it, slots, begin=False):
                for k in range(HS):
                    act.wait_ge(counted, it * HS + k + 1)
                    copy_counts(k).then_inc(counts_copied, 1)
                    if k < HS - 1:
                        place_indices(it + 1, [slot for slot in slots if slot // SP == k])
                if begin:
                    act.wait_ge(h_split, 2)
                    nc.scalar.copy(h_part[1][:], h_all[:]).then_inc(h_split, 1)
                further_windows(it)
                place_indices(it + 1, [slot for slot in slots if slot // SP == HS - 1])

            head_round(0, range(S), begin=True)
            with act.Fori(1, HR - 1) as it:
                head_round(it, range(S))
            head_round(HR - 1, range(LEFT + 1))

            act.wait_ge(weights_loaded, 64)

            def add_bias(s, nth, n):
                act.wait_ge(wide_ready[s], nth)
                if not first(nth):
                    act.wait_ge(hid_ready[s], nth - 1)
                nc.scalar.activation(biased[:, s, 0:n], wide_ps[s][:, 0:n], ACT.Identity,
                                     bias=b1_sb[:, 0:1]).then_inc(biased_ready[s], 1)

            add_bias(0, 1, G)
            add_bias(1, 1, G)
            with act.Fori(1, NC // 2) as j:
                for s in range(2):
                    add_bias(s, j + 1, G)
            add_bias(0, NC // 2 + 1, G)

        @block.vector
        def _(dve):
            for slot in range(S + HS):
                dve.sem_inc(slot_free[slot], 1)
            dve.sem_inc(added, 1 + HS)
            dve.wait_ge(iota_ready, 1)
            nc.vector.tensor_copy(iota_ps[:, 0:WIN], iota_sb[:]).then_inc(iota_placed, 1)

            def scale_of(q, r0, r1, p1):
                dve.wait_ge(std_ready, q + 1)
                nc.vector.reciprocal(rstd[0:p1, r0:r1], std[0:p1, r0:r1]).then_inc(rstd_done, 1)
                dve.wait_ge(rstd_done, q + 1)
                nc.vector.scalar_tensor_tensor(out=shift[0:p1, r0:r1], in0=mean2[0:p1, r0:r1], scalar=-0.5,
                                               in1=rstd[0:p1, r0:r1], op0=ALU.mult,
                                               op1=ALU.mult).then_inc(norm_ready, 1)

            def aggregate(chunks, r0, r1, p1):
                half = stats[0:p1, r0:r1, :]
                dve.wait_ge(stats_done, chunks)
                nc.vector.tensor_tensor(mean2[0:p1, r0:r1], half[:, :, 1], half[:, :, 4], ALU.add)
                nc.vector.tensor_tensor(apart[0:p1, r0:r1], half[:, :, 1], half[:, :, 4], ALU.subtract)
                nc.vector.tensor_tensor(varD[0:p1, r0:r1], half[:, :, 2], half[:, :, 5], ALU.add).then_inc(halves_met, 1)
                met[0] += 1
                dve.wait_ge(halves_met, met[0])
                nc.vector.scalar_tensor_tensor(out=apart2[0:p1, r0:r1], in0=apart[0:p1, r0:r1], scalar=D / 4.0,
                                               in1=apart[0:p1, r0:r1], op0=ALU.mult, op1=ALU.mult).then_inc(squared, 1)
                dve.wait_ge(squared, met[0])
                nc.vector.tensor_tensor(varD[0:p1, r0:r1], varD[0:p1, r0:r1], apart2[0:p1, r0:r1],
                                        ALU.add).then_inc(moments_ready, 1)

            met = [0]
            for q in range(LOADS):
                dve.wait_ge(x_loaded[q], 16)
                with dve.Fori(q * CL, (q + 1) * CL) as c:
                    for u in range(U):
                        last = nc.vector.bn_stats(stats[:, bass.ds(c * U + u, 1), :].rearrange("p a k -> p (a k)"),
                                                  x_all[:, bass.ds(c * G + u * D, D)])
                    last.then_inc(stats_done, 1)
                aggregate((q + 1) * CL, q * CL * U, (q + 1) * CL * U, P)
                if q:
                    scale_of(q - 1, (q - 1) * CL * U, q * CL * U, P)
            dve.wait_ge(x_rest_loaded, 16)
            nc.vector.bn_stats(stats[0:NT, R - 1, :], x_all[0:NT, NC * G:NC * G + D]).then_inc(stats_done, 1)
            aggregate(NC + 1, R - 1, R, NT)
            scale_of(LOADS - 1, (LOADS - 1) * CL * U, LOADS * CL * U, P)
            scale_of(LOADS, R - 1, R, NT)

            dve.wait_ge(src_loaded, 16 * ROW_LOADS)
            nc.vector.tensor_copy(src_f[:], src_i[:]).then_inc(src_floats, 1)

            dve.wait_ge(dst_loaded, 16 * ROW_LOADS)
            nc.vector.tensor_copy(dst_f[:], dst_i[:]).then_inc(dst_floats, 1)
            dve.wait_ge(dst_floats, 1)
            nc.vector.tensor_reduce(lo[:], dst_f[:], AX.X, ALU.min)
            nc.vector.tensor_reduce(hi[:], dst_f[:], AX.X, ALU.max).then_inc(bounds_ready, 1)
            dve.wait_ge(bounds_ready, 1)
            nc.vector.tensor_tensor(spread[:], hi[:], lo[:], ALU.subtract).then_inc(spread_ready, 1)
            dve.wait_ge(ident_ready, 1)
            dve.wait_ge(spread_ready, 1)
            for half in range(2):
                nc.vector.tensor_scalar(lo_diag[:, half, :], ident[0:NH, 0:NH], lo[:, half:half + 1], None, ALU.mult)
                last = nc.vector.tensor_scalar(spread_diag[:, half, :], ident[0:NH, 0:NH],
                                               spread[:, half:half + 1], None, ALU.mult)
            last.then_inc(diags_ready, 1)
            dve.wait_ge(base_copied, 1)
            dve.wait_ge(dst_turned, 1)
            for half in range(2):
                nc.vector.tensor_tensor(
                    dst_rel[:, half * NH * U:(half + 1) * NH * U].rearrange("p (g u) -> p u g", u=U),
                    dst_ps[half][:, 0:NH * U].rearrange("p (u g) -> p u g", u=U),
                    base_bc[:, half * NH:(half + 1) * NH].unsqueeze(1).to_broadcast([P, U, NH]), ALU.subtract)
            dve.wait_ge(spread_copied, 1)
            nc.vector.tensor_scalar(more_i[:], spread_i[:], WIN.bit_length() - 1, None, ALU.arith_shift_right)

            nc.vector.tensor_reduce(widest[:, 0, :], head_spread[:, 0:HG].rearrange("a (b g) -> a b g", g=HS),
                                    AX.X, ALU.max)
            nc.vector.tensor_reduce(widest[:, 1, :], head_spread[:, HG:HR * Q].rearrange("a (b g) -> a b g", g=S),
                                    AX.X, ALU.max)
            dve.wait_ge(src_all_ready, 1)
            nc.vector.tensor_copy(src_h, src_all[:, 0:HT])
            dve.drain()
            nc.vector.tensor_scalar(head_scaled_i[:, 0:HG], head_spread[:, 0:HG], float(DIV), None, ALU.mult)
            nc.vector.tensor_scalar(widest[:, 0, :], widest[:, 0, :], float(DIV), None, ALU.mult)
            nc.vector.tensor_scalar(part_i[:, 0, :], src_h, U.bit_length() - 1, P - 1,
                                    ALU.arith_shift_right, ALU.bitwise_and)
            nc.vector.tensor_scalar(part_i[:, 1, :], src_h, G.bit_length() - 1, None, ALU.arith_shift_right)
            nc.vector.tensor_scalar(part_i[:, 2, :], src_h, U - 1, None, ALU.bitwise_and)
            nc.vector.tensor_scalar(in_tail, src_all[:, 0:HT], float(NC * G), None, ALU.is_ge)
            dve.drain()
            nc.vector.scalar_tensor_tensor(out=head_scaled_i[:, HG:HG + HR], in0=widest[:, 1, :],
                                           scalar=65536.0 / WIN, in1=widest[:, 0, :], op0=ALU.mult, op1=ALU.max)
            dve.drain()
            nc.vector.tensor_scalar(head_more_i[:], head_scaled_i[:], 16, None, ALU.arith_shift_right)
            nc.vector.tensor_copy(parts, part_i)
            dve.drain()
            nc.vector.scalar_tensor_tensor(out=tail_diff[:, 0, :], in0=src_all[:, 0:HT], scalar=-float(NC * G),
                                           in1=parts[:, 0, :], op0=ALU.add, op1=ALU.subtract)
            nc.vector.scalar_tensor_tensor(out=high_key[:], in0=parts[:, 1, :], scalar=float(U),
                                           in1=parts[:, 2, :], op0=ALU.mult, op1=ALU.add)
            dve.drain()
            nc.vector.tensor_tensor(tail_diff[:, 0, :], tail_diff[:, 0, :], in_tail, ALU.mult)
            nc.vector.tensor_scalar(tail_diff[:, 1, :], high_key[:], -1.0, float(HI - 1), ALU.mult, ALU.add)
            dve.drain()
            nc.vector.tensor_tensor(low[:], parts[:, 0, :], tail_diff[:, 0, :], ALU.add)
            nc.vector.tensor_tensor(tail_diff[:, 1, :], tail_diff[:, 1, :], in_tail, ALU.mult)
            dve.drain()
            nc.vector.tensor_tensor(high_key[:], high_key[:], tail_diff[:, 1, :], ALU.add)
            dve.drain()
            nc.vector.tensor_scalar(high_key[:], high_key[:], float(HW), 1.0, ALU.mult, ALU.add)
            dve.drain()
            nc.vector.tensor_tensor(pair_key[:], dst_rel[:, 0:HT], high_key[:], ALU.add)
            dve.drain()
            nc.vector.scalar_tensor_tensor(out=pair_key[:], in0=dst_rel[:, 0:HT], scalar=float(HW), in1=pair_key[:],
                                           op0=ALU.is_lt, op1=ALU.mult)
            dve.drain()
            nc.vector.tensor_scalar(pair_key[:], pair_key[:], -1.0, None, ALU.add).then_inc(tables_ready, 1)
            dve.wait_ge(tables_ready, 1)
            dve.wait_ge(iota_placed, 1)
            dve.wait_ge(head_consts_ready, 1)

            more_count = dve.alloc_register("dve_more_count")
            dve.reg_mov(more_count, 0)
            head_count = dve.alloc_register("dve_head_count")
            dve.reg_mov(head_count, 0)

            def build_onehot(g, half):
                nc.vector.tensor_tensor(
                    onehot[:, half, :].rearrange("p (u n) -> p u n", u=U),
                    iota_ps[:, 0:WIN].unsqueeze(1).to_broadcast([P, U, WIN]),
                    dst_rel[:, bass.ds(g * U, U)].unsqueeze(2).to_broadcast([P, U, WIN]),
                    ALU.is_equal).then_inc(onehot_ready, 1)

            def hot_pair(u, key, lo):
                nc.vector.tensor_scalar(low_hot[:, u, :], iota_lo[:], lo, None, ALU.is_equal)
                return nc.vector.tensor_scalar(pair_hot[:, u, :], iota_z[:], key, None, ALU.is_equal)

            def build_pair(g, u):
                t = g * U + u
                hot_pair(u, pair_key[:, bass.ds(t, 1)], low[:, bass.ds(t, 1)]).then_inc(pair_ready, 1)

            def add_sums(base, sums, width, before):
                dve.wait_ge(added, before)
                nc.vector.tensor_tensor(accT[:, bass.ds(base, width)], accT[:, bass.ds(base, width)],
                                        sums, ALU.add).then_inc(added, 1)

            def base_of(g):
                return dve.value_load(base_i[0:1, bass.ds(g, 1)], min_val=0, max_val=N - 1)

            def bases_of(g, n):
                _, values = nc.values_load_multi_w_load_instructions(
                    base_i[0:1, bass.ds(g, n)], engines=[mybir.EngineType.DVE], min_val=0, max_val=N - 1)
                return values

            def add_group(g, slot, pos, half, base, before, quick):
                dve.wait_ge(sum_ready, pos + 1)
                add_sums(base, sum_ps[half][:, 0:WIN], WIN, before)
                if not quick:
                    group_windows(g, base)
                dve.sem_inc(slot_free[slot], 1)

            def group_windows(g, base):
                more = dve.value_load(more_i[0:1, bass.ds(g, 1)], min_val=0, max_val=(N - 1) // WIN)
                with dve.If(more > 0):
                    nc.vector.tensor_copy(rel_more[:], dst_rel[:, bass.ds(g * U, U)])
                    with dve.Fori(0, more) as k:
                        dve.drain()
                        nc.vector.tensor_scalar(rel_more[:], rel_more[:], -float(WIN), None, ALU.add)
                        dve.drain()
                        for u in range(U):
                            last = nc.vector.tensor_scalar(onehot_more[:, u * WIN:(u + 1) * WIN],
                                                           iota_ps[:, 0:WIN], rel_more[:, u:u + 1], None,
                                                           ALU.is_equal)
                        last.then_inc(more_onehot_ready, 1)
                        dve.reg_add(more_count, more_count, 1)
                        at = nc.s_assert_within(dve.snap(base + k * WIN + WIN), 0, N - 1)
                        dve.wait_ge(more_sum_ready, dve.snap(more_count))
                        nc.vector.tensor_tensor(accT[:, bass.ds(at, WIN)], accT[:, bass.ds(at, WIN)],
                                                extra_ps[:, 0:WIN], ALU.add)
                    dve.drain()

            def further_windows(it):
                if True:
                    with dve.Fori(0, HS) as k:
                        more = dve.value_load(head_more_i[0:1, bass.ds(it * HS + k, 1)], min_val=0, max_val=MORE_MAX)
                        base = dve.value_load(base_i[0:1, bass.ds(it * HS + k, 1)], min_val=0, max_val=N - 1)
                        with dve.If(more > 0):
                            dve.drain()
                            nc.vector.tensor_copy(dst_more[:], dst_rel[:, bass.ds((it * HS + k) * U, U)])
                            with dve.Fori(0, more) as w:
                                dve.drain()
                                nc.vector.tensor_scalar(dst_more[:], dst_more[:], -float(HW), None, ALU.add)
                                dve.drain()
                                nc.vector.tensor_scalar(in_more[:], dst_more[:], 0.0, None, ALU.is_ge)
                                nc.vector.tensor_tensor(key_more[:], dst_more[:],
                                                        high_key[:, bass.ds((it * HS + k) * U, U)], ALU.add)
                                dve.drain()
                                nc.vector.scalar_tensor_tensor(out=key_more[:], in0=dst_more[:], scalar=float(HW),
                                                               in1=key_more[:], op0=ALU.is_lt, op1=ALU.mult)
                                dve.drain()
                                nc.vector.tensor_tensor(key_more[:], key_more[:], in_more[:], ALU.mult)
                                dve.drain()
                                nc.vector.tensor_scalar(key_more[:], key_more[:], -1.0, None, ALU.add)
                                dve.drain()
                                for u in range(U):
                                    last = hot_pair(u, key_more[:, u:u + 1],
                                                    low[:, bass.ds((it * HS + k) * U + u, 1)])
                                last.then_inc(more_pair_ready, 1)
                                dve.reg_add(head_count, head_count, 1)
                                at = nc.s_assert_within(dve.snap(base + w * HW + HW), 0, N - 1 + 2 * HW)
                                dve.wait_ge(more_window_ready, dve.snap(head_count))
                                nc.vector.tensor_tensor(accT[:, bass.ds(at, HW)], accT[:, bass.ds(at, HW)],
                                                        extra_ps[:, 0:HW], ALU.add)
                    dve.drain()

            def head_round(it, begin, quick):
                other_bases = bases_of(HG + it * S, SP * HS)
                head_bases = bases_of(it * HS, HS)
                last_bases = None if begin else bases_of(it * HS - HS, HS)
                before = it * ADDS + 1 + (HS if begin else 0)
                adds = 0

                def add(p):
                    slot = ORDER[p]
                    add_group(group_of(it, slot), slot, it * Q + p, p % 2,
                              other_bases[slot] if slot < S else head_bases[slot - S], before + adds, quick)

                for p, slot in enumerate(ORDER):
                    build_onehot(group_of(it, slot), p % 2)
                    if not begin and W0 <= p < W0 + HS:
                        k = p - W0
                        if k == 0:
                            dve.wait_ge(window_ready, it)
                        add_sums(last_bases[k], win_ps[:, k * HW:(k + 1) * HW], HW, before + adds)
                        adds += 1
                    for u in TILES[p % RS]:
                        build_pair(it * HS + p // RS, u)
                    if p:
                        add(p - 1)
                        adds += 1
                add(Q - 1)
                if not quick:
                    further_windows(it)

            def any_round(it, begin):
                more = dve.value_load(head_more_i[0:1, bass.ds(HG + it, 1)], min_val=0, max_val=MORE_MAX)
                with dve.If(more > 0):
                    head_round(it, begin, False)
                with dve.Else():
                    head_round(it, begin, True)

            def split_h():
                dve.wait_ge(hT_ready, NC + 1)
                dve.wait_ge(h_stored, 16 * (NC + 1))
                dve.wait_ge(h_split, 1)
                nc.vector.tensor_tensor(h_all[:], h_all[:], h_part[0][:], ALU.subtract).then_inc(h_split, 1)
                dve.wait_ge(h_split, 3)
                nc.vector.tensor_tensor(h_part[2][:], h_all[:], h_part[1][:], ALU.subtract).then_inc(h_split, 1)

            dve.wait_ge(acc_started, NC + 1)
            any_round(0, True)
            split_h()
            with dve.Fori(1, HR) as it:
                any_round(it, False)
            adds = HR * ADDS + 1
            for slot in range(LEFT + 1):
                build_onehot(group_of(HR, slot), slot % 2)
                if slot < HS:
                    if slot == 0:
                        dve.wait_ge(window_ready, HR)
                    add_sums(base_of((HR - 1) * HS + slot), win_ps[:, slot * HW:(slot + 1) * HW], HW, adds)
                    adds += 1
                if slot:
                    before = slot - 1
                    add_group(group_of(HR, before), before, HR * Q + before, before % 2,
                              base_of(group_of(HR, before)), adds, False)
                    adds += 1
            add_group(NG, LEFT, HR * Q + LEFT, LEFT % 2, base_of(NG), adds, False)
            dve.drain().then_inc(acc_done, 1)

            def leaky_relu(s, nth, n):
                dve.wait_ge(biased_ready[s], nth)
                if not first(nth):
                    dve.wait_ge(y_ps_ready[s], nth - 1)
                nc.vector.scalar_tensor_tensor(out=hidT[:, s, 0:n], in0=biased[:, s, 0:n], scalar=0.01,
                                               in1=biased[:, s, 0:n], op0=ALU.mult,
                                               op1=ALU.max).then_inc(hid_ready[s], 1)

            def finish(c, s, nth, n, w):
                dve.wait_ge(y_ps_ready[s], nth)
                if not first(nth):
                    dve.wait_ge(y_stored[s], 16 * (nth - 1))
                dve.wait_ge(xb_ready, c + 1)
                nc.vector.tensor_tensor(y_sb[0:n, s, 0:w], sum_ps[s][0:n, 0:w],
                                        x_all[0:n, bass.ds(c * G, w)], ALU.add).then_inc(y_ready[s], 1)

            def finish_pair(j):
                leaky_relu(1, j + 1, G)
                finish(j * 2, 0, j + 1, P, G)
                leaky_relu(0, j + 2, G)
                finish(j * 2 + 1, 1, j + 1, P, G)

            leaky_relu(0, 1, G)
            finish_pair(0)
            with dve.Fori(1, NC // 2) as j:
                finish_pair(j)
            finish(NC, 0, NC // 2 + 1, NT, D)

        @block.tensor
        def _(pe):
            pe.wait_ge(ident_ready, 1)

            def turn_rows(table, halves):
                for half in range(2):
                    for u in range(U):
                        last = nc.tensor.transpose(halves[half][:, u * NH:(u + 1) * NH], table[:, half, u:G:U],
                                                   ident[0:NH, 0:NH])
                return last

            pe.wait_ge(src_floats, 1)
            turn_rows(src_f, src_ps).then_inc(src_turned, 1)
            pe.wait_ge(dst_floats, 1)
            turn_rows(dst_f, dst_ps).then_inc(dst_turned, 1)
            pe.wait_ge(consts_ready, 1)
            pe.wait_ge(diags_ready, 1)
            nc.tensor.matmul(row_ps[:, 0:2 * NH], ones[0:NH, :], lo_diag[:].rearrange("k a g -> k (a g)"),
                             start=True, stop=True)
            nc.tensor.matmul(row_ps[:, 2 * NH:4 * NH], ones[0:NH, :], spread_diag[:].rearrange("k a g -> k (a g)"),
                             start=True, stop=True).then_inc(rows_ready, 1)

            pe.wait_ge(spread_copied, 1)
            for c in range(NC):
                pe.wait_ge(h_ready, c + 1)
                if c >= 2:
                    pe.wait_ge(acc_started, c - 1)
                for u in range(U):
                    last = nc.tensor.transpose(turn_ps[c % 2][:, u * P:(u + 1) * P],
                                               h_all[:, c * G + u * D:c * G + (u + 1) * D], ident[:])
                last.then_inc(hT_ready, 1)
            pe.wait_ge(h_ready, NC + 1)
            pe.wait_ge(acc_started, NC - 1)
            nc.tensor.transpose(turn_ps[0][:, 0:NT], h_all[0:NT, NC * G:NC * G + D],
                                ident[0:NT, 0:NT]).then_inc(hT_ready, 1)
            pe.wait_ge(src_all_ready, 1)
            pe.wait_ge(base_copied, 1)
            pe.wait_ge(acc_started, NC + 1)

            pe.wait_ge(tables_ready, 1)
            more_count = pe.alloc_register("pe_more_count")
            pe.reg_mov(more_count, 0)

            head_count = pe.alloc_register("pe_head_count")
            pe.reg_mov(head_count, 0)

            def sum_slot(into, hot, slot, p1):
                for u in range(U):
                    last = nc.tensor.matmul(into[:, 0:WIN], edges[0:p1, slot, u * D:(u + 1) * D],
                                            hot[0:p1, u * WIN:(u + 1) * WIN],
                                            start=(u == 0), stop=(u == U - 1))
                return last

            def sum_group(g, slot, nth, pos, half, p1=P, quick=False):
                more = None if quick else pe.value_load(more_i[0:1, bass.ds(g, 1)], min_val=0, max_val=(N - 1) // WIN)
                pe.wait_ge(onehot_ready, pos + 1)
                if slot < S:
                    pe.wait_ge(rows_gathered[slot], 16 * U * nth)
                else:
                    pe.wait_ge(edges_loaded[slot], 16 * nth)
                sum_slot(sum_ps[half], onehot[:, half, :], slot, p1).then_inc(sum_ready, 1)
                if quick:
                    return
                with pe.If(more > 0):
                    with pe.Fori(0, more):
                        pe.reg_add(more_count, more_count, 1)
                        pe.wait_ge(more_onehot_ready, pe.snap(more_count))
                        sum_slot(extra_ps, onehot_more[:], slot, p1).then_inc(more_sum_ready, 1)

            banks = [(c, min(512, ZW - c)) for c in range(0, ZW, 512)]

            def count_pairs(u):
                for c, w in banks:
                    last = nc.tensor.matmul(a_ps[:, c:c + w], low_hot[:, u, :], pair_hot[:, u, c:c + w],
                                            start=(u == 0), stop=True, skip_group_check=True)
                return last

            def window_product(into, heads):
                for t in range(HI):
                    for k, part in enumerate(h_part):
                        last = nc.tensor.matmul(into[:, 0:heads * HW], part[:, t * D:(t + 1) * D],
                                                counts[:, t, 0:heads, :],
                                                start=(t == 0 and k == 0), stop=(t == HI - 1 and k == 2))
                return last

            def further_windows(it):
                if True:
                    with pe.Fori(0, HS) as k:
                        more = pe.value_load(head_more_i[0:1, bass.ds(it * HS + k, 1)], min_val=0, max_val=MORE_MAX)
                        with pe.If(more > 0):
                            with pe.Fori(0, more):
                                pe.reg_add(head_count, head_count, 1)
                                pe.wait_ge(more_pair_ready, pe.snap(head_count))
                                for u in range(U):
                                    last = count_pairs(u)
                                last.then_inc(more_counted, 1)
                                pe.wait_ge(more_copied, pe.snap(head_count))
                                window_product(extra_ps, 1).then_inc(more_window_ready, 1)

            def sum_and_count(it, quick):
                for p, slot in enumerate(ORDER):
                    sum_group(group_of(it, slot), slot, it + 1, it * Q + p, p % 2, quick=quick)
                    k = p // RS
                    for u in TILES[p % RS]:
                        pe.wait_ge(pair_ready, (it * HS + k) * U + u + 1)
                        if u == 0 and k:
                            pe.wait_ge(counts_copied, it * HS + k)
                        last = count_pairs(u)
                        if u == U - 1:
                            last.then_inc(counted, 1)

            def heads_product(it):
                pe.wait_ge(h_split, 4)
                pe.wait_ge(counts_copied, (it + 1) * HS)
                pe.wait_ge(added, it * ADDS + 1 + HS + W0 + HS - 2)
                window_product(win_ps, HS).then_inc(window_ready, 1)

            with pe.Fori(0, HR) as it:
                more = pe.value_load(head_more_i[0:1, bass.ds(HG + it, 1)], min_val=0, max_val=MORE_MAX)
                with pe.If(more > 0):
                    sum_and_count(it, False)
                    heads_product(it)
                    further_windows(it)
                with pe.Else():
                    sum_and_count(it, True)
                    heads_product(it)
            for slot in range(LEFT):
                sum_group(group_of(HR, slot), slot, HR + 1, HR * Q + slot, slot % 2)
            sum_group(NG, LEFT, HR + 1, HR * Q + LEFT, LEFT % 2, PT)

            pe.wait_ge(acc_done, 1)
            pe.wait_ge(weights_loaded, 64)

            def first_layer(c, s, nth):
                if not first(nth):
                    pe.wait_ge(biased_ready[s], nth - 1)
                nc.tensor.matmul(wide_ps[s], w1_sb[:], accT[:, bass.ds(c * G, G)],
                                 start=True, stop=True).then_inc(wide_ready[s], 1)

            def second_layer(s, nth, tiles):
                pe.wait_ge(hid_ready[s], nth)
                if not first(nth):
                    pe.wait_ge(y_ready[s], nth - 1)
                for at, (n, nodes) in enumerate(tiles):
                    last = nc.tensor.matmul(sum_ps[s][0:n, at * D:(at + 1) * D], nodes, w2_sb[:],
                                            start=True, stop=True)
                last.then_inc(y_ps_ready[s], 1)

            def tiles_of(s):
                return [(P, hidT[:, s, u:G:U]) for u in range(U)]

            def layer_pair(j):
                first_layer(j * 2 + 1, 1, j + 1)
                second_layer(0, j + 1, tiles_of(0))
                first_layer(j * 2 + 2, 0, j + 2)
                second_layer(1, j + 1, tiles_of(1))

            first_layer(0, 0, 1)
            layer_pair(0)
            with pe.Fori(1, NC // 2) as j:
                layer_pair(j)
            second_layer(0, NC // 2 + 1, [(NT, hidT[:, 0, 0:NT])])


_INS = ["x", "src", "dst", "edge_attr_128", "L0_gnn_W1", "L0_gnn_b1", "L0_gnn_W2", "L0_gnn_b2"]


def kernel(**inputs):
    import numpy as _np
    import concourse.bacc as _bacc
    from concourse import mybir as _mybir
    from concourse.bass_utils import run_bass_kernel_spmd as _run

    nc = _bacc.Bacc("TRN2", target_bir_lowering=False, num_devices=1)
    arrays, args = {}, []
    for name in _INS:
        a = _np.ascontiguousarray(inputs[name])
        arrays[f"in_{name}"] = a
        args.append(nc.dram_tensor(f"in_{name}", a.shape, _mybir.dt.from_np(a.dtype), kind="ExternalInput").ap())
    shape = inputs["x"].shape
    args.append(nc.dram_tensor("out_0", shape, _mybir.dt.float32, kind="ExternalOutput").ap())
    gnn_preln_kernel(nc, *args)
    r = _run(nc, [arrays], core_ids=[0])
    return r.results[0]["out_0"]
```

```python
import concourse.bass as bass
from concourse import mybir
from collections import namedtuple
from contextlib import ExitStack

Run = namedtuple("Run", "n hs hm s hw ring q order tiles before_hs round0 head0 pos0 adds0 nth0")


def gnn_preln_kernel(nc, x, src, dst, edge_attr, w1, b1, w2, b2, out):
    f32, i32, u32, bf16 = mybir.dt.float32, mybir.dt.int32, mybir.dt.uint32, mybir.dt.bfloat16
    ALU, ACT, AX = mybir.AluOpType, mybir.ActivationFunctionType, mybir.AxisListType

    N, D = x.shape
    E = src.shape[0]
    P = 128
    U = 4
    G = P * U
    NG = E // G
    ET = E - NG * G
    PT = ET // U
    assert PT * U == ET and PT > 0
    S = 8
    HM = 4
    RUNS = [(2, 8, 4, S, 8, 8, ((0, 1), (2, 3))),
            (2, 8, 4, S, 12, 8, ((0, 1), (2, 3))),
            (1, 8, 4, S, 17, 4, ((0, 1), (2, 3))),
            (1, 6, 3, S, 17, 4, ((0, 1), (2, 3))),
            (1, 6, 3, S, 19, 4, ((), (0, 1, 2, 3))),
            (2, 6, 3, S, 23, 4, ((), (0, 1, 2, 3))),
            (4, 4, 4, S, 31, 4, ((0, 1), (2, 3))),
            (1, 3, 3, S // 2, 31, 4, ((0, 1), (2, 3)))]
    W0 = 3

    HOTS = 3
    ACT_RUNS = 2
    ACT_FROM = HOTS
    LAG = HOTS - 1

    def plan():
        runs, round0, head0, pos0, adds0, before_hs = [], 0, 0, 0, 1, 0
        nth0 = [0] * HM
        for n, hs, hm, others_of_round, hw, ring, at_places in RUNS:
            order, tiles = [], []
            for k in range(hs):
                others = range(k * others_of_round // hs, (k + 1) * others_of_round // hs)
                order += [S + k % hm, *others]
                tiles += [(k, *tiles_of_place) for tiles_of_place in at_places] + [(k,)] * (len(others) - 1)
            q = len(order)
            assert hs % hm == 0 and hs * U % ring == 0 and W0 + max(hs, before_hs) <= q
            runs.append(Run(n, hs, hm, others_of_round, hw, ring, q, order, tiles, before_hs, round0, head0, pos0,
                            adds0, list(nth0)))
            round0, head0, pos0 = round0 + n, head0 + n * hs, pos0 + n * q
            adds0, before_hs = adds0 + q + before_hs + (n - 1) * (q + hs), hs
            nth0 = [use + (n * (hs // hm) if at < hm else 0) for at, use in enumerate(nth0)]
        return runs, round0, head0, pos0, adds0

    PLAN, HR, HG, POS, ADDS = plan()
    HT = HG * U
    assert all(len(at_place) > 1 for run in PLAN[:ACT_RUNS] for at_place in run.tiles)
    IN_ROUNDS = HG + HR * S
    LEFT = NG - IN_ROUNDS
    assert 0 <= LEFT < PLAN[-1].s and all(run.s == S for run in PLAN[:-1]) and PLAN[-1].n == 1
    TAIL = ([(slot, HR, HG + (HR - 1) * S + slot) for slot in range(PLAN[-1].s, S)]
            + [(slot, HR + 1, IN_ROUNDS + slot) for slot in range(LEFT + 1)])
    NH = (NG + 1) // 2
    assert NH * 2 == NG + 1 and NH <= P
    WIN = 128
    NC = N // G
    NT = N - NC * G
    assert 0 < NT <= P and NC % 4 == 0
    LOADS = 4
    CL = NC // LOADS
    R = NC * U + 1
    ROW_LOADS = 2 + -(-G // ET)
    HI = R
    HW = max(run.hw for run in PLAN)
    ZW = HI * HW
    NP = 7
    PW = HI * D // NP
    EARLY = 3
    assert PW * NP == HI * D and 2 * NP <= PLAN[0].q

    def scale_of_spread(hw):
        return -(-65536 // hw)

    MORE_MAX = (N - 1) * scale_of_spread(min(run.hw for run in PLAN)) // 65536
    assert ZW <= 3 * 512 and HG <= NH and all(run.hs * run.hw <= 512 for run in PLAN)
    EPS = 1e-5

    def first(nth):
        return isinstance(nth, int) and nth == 1

    def by_scalar(run, p):
        return run in PLAN[:ACT_RUNS] and p >= ACT_FROM and p % 2 == 1

    def act_hots(run):
        return sum(by_scalar(run, p) for p in range(run.q))

    def act_hots_before(run):
        return sum(act_hots(before) * before.n for before in PLAN[:PLAN.index(run)])

    def hots_before(run, i, p):
        return (i * (run.q - act_hots(run))
                + (run.pos0 + p - act_hots_before(run) - sum(by_scalar(run, at) for at in range(p))))

    def other_group(it, slot):
        return HG + it * S + slot

    def places(run, i):
        k = -1
        for p, slot in enumerate(run.order):
            if slot < S:
                yield p, None, slot, run.round0 + i + 1, other_group(run.round0 + i, slot)
            else:
                k += 1
                yield (p, k, slot, run.nth0[slot - S] + i * (run.hs // run.hm) + k // run.hm + 1,
                       run.head0 + i * run.hs + k)

    def adds_before(run, i):
        if isinstance(i, int) and i == 0:
            return run.adds0
        return i * (run.q + run.hs) + (run.adds0 + run.before_hs - run.hs)

    h_rows = nc.dram_tensor("h_rows", (N, D), f32).ap()

    x_chunks = x[0:NC * G, :].rearrange("(c p u) d -> p c (u d)", p=P, u=U)
    h_chunks = h_rows[0:NC * G, :].rearrange("(c p u) d -> c p (u d)", p=P, u=U)
    out_chunks = out[0:NC * G, :].rearrange("(c p u) d -> c p (u d)", p=P, u=U)
    edge_groups = edge_attr[0:NG * G, :].rearrange("(g p u) d -> g p (u d)", p=P, u=U)
    edge_rest = edge_attr[NG * G:E, :].rearrange("(p u) d -> p (u d)", u=U)

    with ExitStack() as ctx:
        def sb(name, shape, dt=f32):
            return ctx.enter_context(nc.sbuf_tensor(name, shape, dt))

        def sem(name):
            return ctx.enter_context(nc.semaphore(name))

        def sems(name, n):
            return [sem(f"{name}{i}") for i in range(n)]

        x_all = sb("x_all", [P, R * D])
        h_all = sb("h_all", [P, R * D])
        accT = sb("accT", [P, (NC + 1) * G])
        stats = sb("stats", [P, R, 6])
        mean2 = sb("mean2", [P, R])
        apart = sb("apart", [P, R])
        apart2 = sb("apart2", [P, R])
        varD = sb("varD", [P, R])
        std = sb("std", [P, R])
        rstd = sb("rstd", [P, R])
        shift = sb("shift", [P, R])
        eps = sb("eps", [P, 1])
        ident = sb("ident", [P, P])
        ones = sb("ones", [P, P])
        iota_sb = sb("iota_sb", [P, WIN])
        tables_i = sb("tables_i", [P, 4, G], i32)
        src_i, dst_i = tables_i[0:NH, 0:2, :], tables_i[0:NH, 2:4, :]
        lo = sb("lo", [NH, 2])
        hi = sb("hi", [NH, 2])
        spread = sb("spread", [NH, 2])
        lo_diag = sb("lo_diag", [NH, 2, NH])
        spread_diag = sb("spread_diag", [NH, 2, NH])
        base_bc = sb("base_bc", [P, 2 * NH])
        base_i = sb("base_i", [1, 2 * NH], i32)
        other_base_i = sb("other_base_i", [1, HR * S], i32)
        spread_i = sb("spread_i", [1, 2 * NH], i32)
        more_i = sb("more_i", [1, 2 * NH], i32)
        src_all = sb("src_all", [P, 2 * NH * U])
        dst_rel = sb("dst_rel", [P, 2 * NH * U])
        idx = sb("idx", [P, S, U], u32)
        edges = sb("edges", [P, S + HM, G])
        onehot = sb("onehot", [P, HOTS, G])
        h_left = sb("h_left", [P, HI * D])
        h_last = sb("h_last", [P, HI * D], bf16)
        tables_f = h_last[:, 0:2 * 4 * G].bitcast(f32).rearrange("p (a w) -> p a w", w=G)
        src_f, dst_f = tables_f[0:NH, 0:2, :], tables_f[0:NH, 2:4, :]
        counts = sb("counts", [P, HI * max(run.hs * run.hw for run in PLAN)], mybir.dt.float16)
        iota_z = sb("iota_z", [P, ZW], mybir.dt.int16)
        iota_lo = sb("iota_lo", [P, P], bf16)
        pair_hot = sb("pair_hot", [P, max(run.ring * HI * run.hw for run in PLAN)], bf16)
        low_hot = sb("low_hot", [P, max(run.ring for run in PLAN), P], bf16)
        low = sb("low", [P, HT])
        high_key = sb("high_key", [P, HT])
        pair_key = sb("pair_key", [P, HT])
        widest = sb("widest", [1, 2, HR])
        head_spread = sb("head_spread", [1, IN_ROUNDS])
        head_scaled_i = sb("head_scaled_i", [1, HG + HR], i32)
        head_more_i = sb("head_more_i", [1, HG + HR], i32)
        dst_more = sb("dst_more", [P, U])
        in_more = sb("in_more", [P, U])
        key_more = sb("key_more", [P, U])
        rel_more = sb("rel_more", [P, U])
        onehot_more = sb("onehot_more", [P, G])
        spare_i = tables_i[:].rearrange("p a w -> p (a w)")[:, 0:4 * HT].rearrange("p (b t) -> p b t", t=HT)
        src_h, part_i = spare_i[:, 0, :], spare_i[:, 1:4, :]
        spare = tables_f.rearrange("p a w -> p (a w)")[:, 0:6 * HT].rearrange("p (b t) -> p b t", t=HT)
        parts, in_tail = spare[:, 0:3, :], spare[:, 3, :]
        tail_diff = spare[:, 4:6, :]
        w1_sb = sb("w1_sb", [D, D])
        w2_sb = sb("w2_sb", [D, D])
        b1_sb = sb("b1_sb", [D, 1])
        b2_bc = sb("b2_bc", [P, D])
        biased, hidT, y_sb = edges[:, 4:6, :], edges[:, 6:8, :], edges[:, 8:10, :]

        def bank(name, width=512):
            return ctx.enter_context(nc.psum_tensor(name, [P, width], f32))

        a_ps = bank("a_ps", 3 * 512)
        sum_ps = [bank(f"sum_ps{k}") for k in range(HOTS)]
        win_ps = bank("win_ps")
        extra_ps = bank("extra_ps")
        a_banks = [a_ps[:, k * 512:(k + 1) * 512] for k in range(3)]
        src_ps, dst_ps, row_ps = a_banks[0:2], sum_ps[0:2], a_banks[2]
        turn_ps = [win_ps, extra_ps]
        wide_ps = a_banks[0:2]

        x_loaded = sems("x_loaded", LOADS)
        x_rest_loaded = sem("x_rest_loaded")
        src_loaded = sem("src_loaded")
        dst_loaded = sem("dst_loaded")
        weights_loaded = sem("weights_loaded")
        iota_ready = sem("iota_ready")
        zeroed = sem("zeroed")
        ident_ready = sem("ident_ready")
        consts_ready = sem("consts_ready")
        h_tail_zeroed = sem("h_tail_zeroed")
        head_consts_ready = sem("head_consts_ready")
        stats_done = sem("stats_done")
        halves_met = sem("halves_met")
        squared = sem("squared")
        moments_ready = sem("moments_ready")
        std_ready = sem("std_ready")
        rstd_done = sem("rstd_done")
        norm_ready = sem("norm_ready")
        h_ready = sem("h_ready")
        h_ready_pool = sem("h_ready_pool")
        h_stored = sem("h_stored")
        hT_ready = sem("hT_ready")
        acc_started = sem("acc_started")
        src_floats = sem("src_floats")
        dst_floats = sem("dst_floats")
        bounds_ready = sem("bounds_ready")
        spread_ready = sem("spread_ready")
        diags_ready = sem("diags_ready")
        src_turned = sem("src_turned")
        dst_turned = sem("dst_turned")
        rows_ready = sem("rows_ready")
        base_copied = sem("base_copied")
        src_all_ready = sem("src_all_ready")
        spread_copied = sem("spread_copied")
        tables_ready = sem("tables_ready")
        xb_ready = sem("xb_ready")

        slot_free = sems("slot_free", S + HM)
        idx_ready = sems("idx_ready", S)
        edges_loaded = sems("edges_loaded", S + HM)
        rows_gathered = sems("rows_gathered", S)
        onehot_ready = sem("onehot_ready")
        act_onehot_ready = sem("act_onehot_ready")
        sum_ready = sem("sum_ready")
        left_ready = sem("left_ready")
        last_ready = sem("last_ready")
        pair_ready = sem("pair_ready")
        counted = sem("counted")
        counts_copied = sem("counts_copied")
        window_ready = sem("window_ready")
        more_pair_ready = sem("more_pair_ready")
        more_counted = sem("more_counted")
        more_copied = sem("more_copied")
        more_window_ready = sem("more_window_ready")
        more_onehot_ready = sem("more_onehot_ready")
        more_sum_ready = sem("more_sum_ready")
        acc_done = sem("acc_done")
        added = sem("added")
        gathers_begun = sem("gathers_begun")

        wide_ready = sems("wide_ready", 2)
        biased_ready = sems("biased_ready", 2)
        hid_ready = sems("hid_ready", 2)
        y_ps_ready = sems("y_ps_ready", 2)
        y_ready = sems("y_ready", 2)
        y_stored = sems("y_stored", 2)

        def run_counts(run):
            return counts[:, 0:HI * run.hs * run.hw].rearrange("p (t k n) -> p t k n", k=run.hs, n=run.hw)

        def pair_buffer(run, tile):
            return pair_hot[:, tile % run.ring * HI * run.hw:(tile % run.ring + 1) * HI * run.hw]

        def sums_of(p):
            return sum_ps[p % HOTS][:, 0:WIN]

        def piece(table, k):
            return table[:, k * PW:(k + 1) * PW]

        def upper_half(values, c0, c1):
            return values[:, c0:c1].bitcast(bf16)[:, 1:2 * (c1 - c0):2]

        block = ctx.enter_context(nc.Block())

        @block.sync
        def _(sp):
            for q in range(LOADS):
                sp.dma_start(x_all[:, q * CL * G:(q + 1) * CL * G].rearrange("p (c w) -> p c w", c=CL),
                             x_chunks[:, q * CL:(q + 1) * CL, :]).then_inc(x_loaded[q], 16)
            sp.dma_start(x_all[0:NT, NC * G:NC * G + D], x[NC * G:N, :]).then_inc(x_rest_loaded, 16)
            with sp.Fori(0, LOADS) as q:
                for k in range(CL):
                    if k < CL - 1:
                        sp.wait_ge(h_ready, q * (CL - 1) + k + 1)
                    else:
                        sp.wait_ge(h_ready_pool, q + 1)
                    sp.dma_start(h_chunks[q * CL + k], h_all[:, bass.ds((q * CL + k) * G, G)]).then_inc(h_stored, 16)
            sp.wait_ge(h_ready, LOADS * (CL - 1) + 1)
            sp.dma_start(h_rows[NC * G:N, :], h_all[0:NT, NC * G:NC * G + D]).then_inc(h_stored, 16)
            def by_free_slot(run, i):
                at = [p for p, slot in enumerate(run.order) if slot >= S]

                def place_before(step):
                    p, k, *_ = step
                    return p - run.q if k is None else at[k - run.hm] - (run.q if k < run.hm else 0)

                return sorted(places(run, i), key=place_before)

            def load_edges(slot, nth, g):
                sp.wait_ge(slot_free[slot], nth)
                sp.dma_start(edges[:, slot, :], edge_groups[g]).then_inc(edges_loaded[slot], 16)

            for run in PLAN:
                with sp.Fori(0, run.n) as i:
                    for _, _, slot, nth, g in by_free_slot(run, i):
                        load_edges(slot, nth, g)
            for slot, nth, g in TAIL[:-1]:
                load_edges(slot, nth, g)
            sp.wait_ge(slot_free[LEFT], HR + 1)
            sp.dma_start(edges[0:PT, LEFT, :], edge_rest).then_inc(edges_loaded[LEFT], 16)
            with sp.Fori(0, NC // 2) as j:
                for s in range(2):
                    sp.wait_ge(y_ready[s], j + 1)
                    sp.dma_start(out_chunks[j * 2 + s], y_sb[:, s, :]).then_inc(y_stored[s], 16)
            sp.wait_ge(y_ready[0], NC // 2 + 1)
            sp.dma_start(out[NC * G:N, :], y_sb[0:NT, 0, 0:D]).then_inc(y_stored[0], 16)
            sp.wait_ge(y_stored[0], 16 * (NC // 2 + 1))
            sp.wait_ge(y_stored[1], 16 * (NC // 2))

        @block.gpsimd
        def _(pool):
            nc.gpsimd.iota(iota_sb[:], [[1, WIN]], base=0, channel_multiplier=0,
                           allow_small_or_imprecise_dtypes=True).then_inc(iota_ready, 1)
            nc.gpsimd.memset(ident[:], 0.0).then_inc(zeroed, 1)
            nc.gpsimd.memset(ones[:], 1.0)
            nc.gpsimd.memset(eps[:], EPS)
            nc.gpsimd.memset(accT[:, N:(NC + 1) * G], 0.0).then_inc(consts_ready, 1)
            nc.gpsimd.iota(iota_z[:], [[1, ZW]], base=0, channel_multiplier=0, allow_small_or_imprecise_dtypes=True)
            nc.gpsimd.iota(iota_lo[:], [[1, P]], base=0, channel_multiplier=0,
                           allow_small_or_imprecise_dtypes=True).then_inc(head_consts_ready, 1)
            nc.gpsimd.memset(h_all[:, NC * G:NC * G + D], 0.0).then_inc(h_tail_zeroed, 1)
            pool.wait_ge(zeroed, 1)
            nc.gpsimd.affine_select(out=ident[:], in_=ident[:], compare_op=ALU.not_equal, fill=1.0, base=0,
                                    pattern=[[-1, P]], channel_multiplier=1).then_inc(ident_ready, 1)
            for q in range(LOADS):
                pool.wait_ge(norm_ready, q + 1)
                for tile in range(((q + 1) * CL - 1) * U, (q + 1) * CL * U):
                    nc.gpsimd.tensor_scalar(h_all[:, tile * D:(tile + 1) * D], x_all[:, tile * D:(tile + 1) * D],
                                            rstd[:, tile:tile + 1], shift[:, tile:tile + 1], ALU.mult, ALU.add)
                pool.drain()
                chunk = h_all[:, ((q + 1) * CL - 1) * G:(q + 1) * CL * G]
                nc.gpsimd.tensor_scalar(chunk, chunk, 0.0, None, ALU.max).then_inc(h_ready_pool, 1)
            pool.wait_ge(h_stored, 16 * (NC + 1))
            def gather(slot, nth, p1):
                pool.wait_ge(idx_ready[slot], nth)
                pool.sem_inc(gathers_begun, 1)
                pool.wait_ge(edges_loaded[slot], 16 * nth)
                pool.sem_inc(gathers_begun, 1)
                for u in range(U):
                    pool.indirect_dma_start(
                        out=edges[0:p1, slot, u * D:(u + 1) * D], out_offset=None, in_=h_rows[:, :],
                        in_offset=bass.IndirectOffsetOnAxis(ap=idx[0:p1, slot, u:u + 1], axis=0),
                        compute_op=ALU.add).then_inc(rows_gathered[slot], 16)

            with pool.Fori(0, HR) as it:
                for slot in range(S):
                    gather(slot, it + 1, P)
            for slot in range(LEFT):
                gather(slot, HR + 1, P)
            gather(LEFT, HR + 1, PT)

            pool.wait_ge(weights_loaded, 64)
            pool.wait_ge(h_ready, LOADS * (CL - 1) + 1)
            with pool.Fori(0, NC) as c:
                nc.gpsimd.tensor_tensor(x_all[:, bass.ds(c * G, G)].rearrange("p (u d) -> p u d", u=U),
                                        x_all[:, bass.ds(c * G, G)].rearrange("p (u d) -> p u d", u=U),
                                        b2_bc[:].unsqueeze(1).to_broadcast([P, U, D]), ALU.add).then_inc(xb_ready, 1)
            nc.gpsimd.tensor_tensor(x_all[0:NT, NC * G:NC * G + D], x_all[0:NT, NC * G:NC * G + D],
                                    b2_bc[0:NT, :], ALU.add).then_inc(xb_ready, 1)

        @block.scalar
        def _(act):
            def load_rows(values, tile, loaded):
                act.dma_start(tile[:, 0, :], values[0:NH * G].rearrange("(g e) -> g e", e=G)).then_inc(loaded, 16)
                act.dma_start(tile[0:NH - 1, 1, :],
                              values[NH * G:NG * G].rearrange("(g e) -> g e", e=G)).then_inc(loaded, 16)
                for at in range(0, G, ET):
                    n = min(ET, G - at)
                    act.dma_start(tile[NH - 1:NH, 1, at:at + n],
                                  values[NG * G:NG * G + n].rearrange("(a e) -> a e", a=1)).then_inc(loaded, 16)

            load_rows(src, src_i, src_loaded)
            load_rows(dst, dst_i, dst_loaded)
            act.dma_start(w1_sb[:], w1).then_inc(weights_loaded, 16)
            act.dma_start(w2_sb[:], w2).then_inc(weights_loaded, 16)
            act.dma_start(b1_sb[:], b1.rearrange("(d a) -> d a", a=1)).then_inc(weights_loaded, 16)
            act.dma_start(b2_bc[:], b2.rearrange("(a d) -> a d", a=1).to_broadcast([P, D])).then_inc(weights_loaded, 16)

            act.wait_ge(consts_ready, 1)

            def deviation(q, r0, r1, p1):
                act.wait_ge(moments_ready, q + 1)
                nc.scalar.activation(std[0:p1, r0:r1], varD[0:p1, r0:r1], ACT.Sqrt, scale=1.0 / D,
                                     bias=eps[0:p1, :]).then_inc(std_ready, 1)

            def normalise(q):
                act.wait_ge(norm_ready, q + 1)
                with act.Fori(q * CL, (q + 1) * CL - 1) as c:
                    for u in range(U):
                        last = nc.scalar.activation(
                            h_all[:, bass.ds(c * G + u * D, D)], x_all[:, bass.ds(c * G + u * D, D)], ACT.Relu,
                            bias=shift[:, bass.ds(c * U + u, 1)], scale=rstd[:, bass.ds(c * U + u, 1)])
                    last.then_inc(h_ready, 1)

            deviation(0, 0, CL * U, P)
            for q in range(1, LOADS):
                deviation(q, q * CL * U, (q + 1) * CL * U, P)
                normalise(q - 1)
            deviation(LOADS, R - 1, R, NT)
            normalise(LOADS - 1)
            act.wait_ge(norm_ready, LOADS + 1)
            act.wait_ge(h_tail_zeroed, 1)
            nc.scalar.activation(h_all[0:NT, NC * G:NC * G + D], x_all[0:NT, NC * G:NC * G + D], ACT.Relu,
                                 bias=shift[0:NT, R - 1:R], scale=rstd[0:NT, R - 1:R]).then_inc(h_ready, 1)

            def place_indices(it, slots):
                for slot in slots:
                    act.wait_ge(slot_free[slot], it + 1)
                    nc.scalar.copy(idx[:, slot, :],
                                   src_all[:, bass.ds(other_group(it, slot) * U, U)]).then_inc(idx_ready[slot], 1)

            act.wait_ge(src_turned, 1)
            for half in range(2):
                last = nc.scalar.copy(
                    src_all[:, half * NH * U:(half + 1) * NH * U].rearrange("p (g u) -> p u g", u=U),
                    src_ps[half][:, 0:NH * U].rearrange("p (u g) -> p u g", u=U))
            last.then_inc(src_all_ready, 1)
            act.wait_ge(src_all_ready, 1)
            place_indices(0, range(S))
            act.wait_ge(rows_ready, 1)
            nc.scalar.copy(base_bc[:], row_ps[:, 0:2 * NH])
            nc.scalar.copy(base_i[:], row_ps[0:1, 0:2 * NH])
            nc.scalar.copy(other_base_i[:], row_ps[0:1, HG:IN_ROUNDS])
            nc.scalar.copy(spread_i[:], row_ps[0:1, 2 * NH:4 * NH]).then_inc(base_copied, 1)
            nc.scalar.copy(head_spread[:], row_ps[0:1, 2 * NH:2 * NH + IN_ROUNDS]).then_inc(spread_copied, 1)
            with act.Fori(0, NC // 2) as j:
                for b in range(2):
                    act.wait_ge(hT_ready, j * 2 + b + 1)
                    nc.scalar.activation(
                        accT[:, bass.ds((j * 2 + b) * G, G)].rearrange("d (p u) -> d u p", u=U),
                        turn_ps[b][:].rearrange("d (u p) -> d u p", u=U), ACT.Copy, scale=2.0,
                    ).then_inc(acc_started, 1)
            act.wait_ge(hT_ready, NC + 1)
            nc.scalar.activation(accT[:, NC * G:N], turn_ps[0][:, 0:NT], ACT.Copy,
                                 scale=2.0).then_inc(acc_started, 1)

            more_count = act.alloc_register("act_more_count")
            act.reg_mov(more_count, 0)
            act.wait_ge(tables_ready, 1)

            def copy_counts(run, k):
                return nc.scalar.copy(run_counts(run)[:, :, k, :],
                                      a_ps[:, 0:HI * run.hw].rearrange("p (t n) -> p t n", n=run.hw))

            def build_onehot(run, i, p, g):
                act.wait_ge(sum_ready, run.pos0 + i * run.q + p - HOTS + 1)
                for u in range(U):
                    nc.scalar.activation(onehot[:, p % HOTS, u * WIN:(u + 1) * WIN], iota_sb[:], ACT.Square,
                                         bias=dst_rel[:, bass.ds(g * U + u, 1)], scale=-1.0)
                act.drain()
                nc.scalar.activation(onehot[:, p % HOTS, :], onehot[:, p % HOTS, :], ACT.Relu,
                                     bias=ones[:, 0:1], scale=-1.0).then_inc(act_onehot_ready, 1)

            def further_windows(run, i):
                wide = act.value_load(head_more_i[0:1, bass.ds(HG + run.round0 + i, 1)], min_val=0, max_val=MORE_MAX)
                with act.If(wide > 0):
                    with act.Fori(0, run.hs) as k:
                        more = act.value_load(head_more_i[0:1, bass.ds(run.head0 + i * run.hs + k, 1)],
                                              min_val=0, max_val=MORE_MAX)
                        with act.If(more > 0):
                            with act.Fori(0, more):
                                act.reg_add(more_count, more_count, 1)
                                act.wait_ge(more_counted, act.snap(more_count))
                                copy_counts(run, 0).then_inc(more_copied, 1)

            def head_round(run, i, slots=range(S)):
                it = run.round0 + i
                steps = list(places(run, i))
                wait_for = 1 if run is PLAN[0] else 0

                def at_head(slot):
                    return min(slot * run.hs // S + wait_for, run.hs - 1)

                for k in range(run.hs):
                    p = 2 * k + HOTS
                    if p < run.q and by_scalar(run, p):
                        build_onehot(run, i, p, steps[p][-1])
                    act.wait_ge(counted, (run.head0 + i * run.hs + k + 1) * U)
                    copy_counts(run, k).then_inc(counts_copied, 1)
                    if k < run.hs - 1:
                        place_indices(it + 1, [slot for slot in slots if at_head(slot) == k])
                further_windows(run, i)
                place_indices(it + 1, [slot for slot in slots if at_head(slot) == run.hs - 1])

            for run in PLAN:
                if run is PLAN[0]:
                    head_round(run, 0)
                if run is not PLAN[-1]:
                    with act.Fori(1 if run is PLAN[0] else 0, run.n) as i:
                        head_round(run, i)
            head_round(PLAN[-1], 0, range(LEFT + 1))

            act.wait_ge(weights_loaded, 64)

            def add_bias(s, nth, n):
                act.wait_ge(wide_ready[s], nth)
                if not first(nth):
                    act.wait_ge(hid_ready[s], nth - 1)
                nc.scalar.activation(biased[:, s, 0:n], wide_ps[s][:, 0:n], ACT.Identity,
                                     bias=b1_sb[:, 0:1]).then_inc(biased_ready[s], 1)

            add_bias(0, 1, G)
            add_bias(1, 1, G)
            with act.Fori(1, NC // 2) as j:
                for s in range(2):
                    add_bias(s, j + 1, G)
            add_bias(0, NC // 2 + 1, G)

        @block.vector
        def _(dve):
            for slot in range(S + HM):
                dve.sem_inc(slot_free[slot], 1)
            dve.sem_inc(added, 1)
            dve.wait_ge(iota_ready, 1)

            def scale_of(q, r0, r1, p1):
                dve.wait_ge(std_ready, q + 1)
                nc.vector.reciprocal(rstd[0:p1, r0:r1], std[0:p1, r0:r1]).then_inc(rstd_done, 1)
                dve.wait_ge(rstd_done, q + 1)
                nc.vector.scalar_tensor_tensor(out=shift[0:p1, r0:r1], in0=mean2[0:p1, r0:r1], scalar=-0.5,
                                               in1=rstd[0:p1, r0:r1], op0=ALU.mult,
                                               op1=ALU.mult).then_inc(norm_ready, 1)

            def aggregate(pieces, r0, r1, p1):
                half = stats[0:p1, r0:r1, :]
                dve.wait_ge(stats_done, pieces)
                nc.vector.tensor_tensor(mean2[0:p1, r0:r1], half[:, :, 1], half[:, :, 4], ALU.add)
                nc.vector.tensor_tensor(apart[0:p1, r0:r1], half[:, :, 1], half[:, :, 4], ALU.subtract)
                nc.vector.tensor_tensor(varD[0:p1, r0:r1], half[:, :, 2], half[:, :, 5],
                                        ALU.add).then_inc(halves_met, 1)
                met[0] += 1
                dve.wait_ge(halves_met, met[0])
                nc.vector.scalar_tensor_tensor(out=apart2[0:p1, r0:r1], in0=apart[0:p1, r0:r1], scalar=D / 4.0,
                                               in1=apart[0:p1, r0:r1], op0=ALU.mult, op1=ALU.mult).then_inc(squared, 1)
                dve.wait_ge(squared, met[0])
                nc.vector.tensor_tensor(varD[0:p1, r0:r1], varD[0:p1, r0:r1], apart2[0:p1, r0:r1],
                                        ALU.add).then_inc(moments_ready, 1)

            met = [0]
            for q in range(LOADS):
                dve.wait_ge(x_loaded[q], 16)
                for tile in range(q * CL * U, (q + 1) * CL * U):
                    last = nc.vector.bn_stats(stats[:, tile, :], x_all[:, tile * D:(tile + 1) * D])
                last.then_inc(stats_done, 1)
                aggregate(q + 1, q * CL * U, (q + 1) * CL * U, P)
                if q:
                    scale_of(q - 1, (q - 1) * CL * U, q * CL * U, P)
            dve.wait_ge(x_rest_loaded, 16)
            nc.vector.bn_stats(stats[0:NT, R - 1, :], x_all[0:NT, NC * G:NC * G + D]).then_inc(stats_done, 1)
            aggregate(LOADS + 1, R - 1, R, NT)
            scale_of(LOADS - 1, (LOADS - 1) * CL * U, LOADS * CL * U, P)
            scale_of(LOADS, R - 1, R, NT)

            dve.wait_ge(src_loaded, 16 * ROW_LOADS)
            nc.vector.tensor_copy(src_f, src_i).then_inc(src_floats, 1)

            dve.wait_ge(dst_loaded, 16 * ROW_LOADS)
            nc.vector.tensor_copy(dst_f, dst_i).then_inc(dst_floats, 1)
            dve.wait_ge(dst_floats, 1)
            nc.vector.tensor_reduce(lo[:], dst_f, AX.X, ALU.min)
            nc.vector.tensor_reduce(hi[:], dst_f, AX.X, ALU.max).then_inc(bounds_ready, 1)
            dve.wait_ge(bounds_ready, 1)
            nc.vector.tensor_tensor(spread[:], hi[:], lo[:], ALU.subtract).then_inc(spread_ready, 1)
            dve.wait_ge(ident_ready, 1)
            dve.wait_ge(spread_ready, 1)
            for half in range(2):
                nc.vector.tensor_scalar(lo_diag[:, half, :], ident[0:NH, 0:NH], lo[:, half:half + 1], None, ALU.mult)
                last = nc.vector.tensor_scalar(spread_diag[:, half, :], ident[0:NH, 0:NH],
                                               spread[:, half:half + 1], None, ALU.mult)
            last.then_inc(diags_ready, 1)

            def take_off_first(k):
                nc.vector.tensor_tensor(piece(h_left, k), piece(h_all, k), upper_half(h_all, k * PW, (k + 1) * PW),
                                        ALU.subtract).then_inc(left_ready, 1)

            dve.wait_ge(h_ready, LOADS * (CL - 1) + 1)
            dve.wait_ge(h_ready_pool, LOADS)
            for k in range(EARLY):
                take_off_first(k)
            dve.wait_ge(base_copied, 1)
            dve.wait_ge(dst_turned, 1)
            for half in range(2):
                nc.vector.tensor_tensor(
                    dst_rel[:, half * NH * U:(half + 1) * NH * U].rearrange("p (g u) -> p u g", u=U),
                    dst_ps[half][:, 0:NH * U].rearrange("p (u g) -> p u g", u=U),
                    base_bc[:, half * NH:(half + 1) * NH].unsqueeze(1).to_broadcast([P, U, NH]), ALU.subtract)
            dve.wait_ge(spread_copied, 1)
            nc.vector.tensor_scalar(more_i[:], spread_i[:], WIN.bit_length() - 1, None, ALU.arith_shift_right)

            for run in PLAN:
                r0, r1 = run.round0, run.round0 + run.n
                for k, g0, size in ((0, run.head0, run.hs), (1, HG + r0 * S, run.s)):
                    nc.vector.tensor_reduce(
                        widest[:, k, r0:r1],
                        head_spread[:, g0:g0 + run.n * size].rearrange("a (b g) -> a b g", g=size), AX.X, ALU.max)
            dve.wait_ge(src_all_ready, 1)
            nc.vector.tensor_copy(src_h, src_all[:, 0:HT])
            dve.drain()
            for run in PLAN:
                g0, g1, r0, r1 = run.head0, run.head0 + run.n * run.hs, run.round0, run.round0 + run.n
                scale = float(scale_of_spread(run.hw))
                nc.vector.tensor_scalar(head_scaled_i[:, g0:g1], head_spread[:, g0:g1], scale, None, ALU.mult)
                nc.vector.tensor_scalar(widest[:, 0, r0:r1], widest[:, 0, r0:r1], scale, None, ALU.mult)
            nc.vector.tensor_scalar(part_i[:, 0, :], src_h, U.bit_length() - 1, P - 1,
                                    ALU.arith_shift_right, ALU.bitwise_and)
            nc.vector.tensor_scalar(part_i[:, 1, :], src_h, G.bit_length() - 1, None, ALU.arith_shift_right)
            nc.vector.tensor_scalar(part_i[:, 2, :], src_h, U - 1, None, ALU.bitwise_and)
            nc.vector.tensor_scalar(in_tail, src_all[:, 0:HT], float(NC * G), None, ALU.is_ge)
            dve.drain()
            nc.vector.scalar_tensor_tensor(out=head_scaled_i[:, HG:HG + HR], in0=widest[:, 1, :],
                                           scalar=65536.0 / WIN, in1=widest[:, 0, :], op0=ALU.mult, op1=ALU.max)
            dve.drain()
            nc.vector.tensor_scalar(head_more_i[:], head_scaled_i[:], 16, None, ALU.arith_shift_right)
            nc.vector.tensor_copy(parts, part_i)
            dve.drain()
            nc.vector.scalar_tensor_tensor(out=tail_diff[:, 0, :], in0=src_all[:, 0:HT], scalar=-float(NC * G),
                                           in1=parts[:, 0, :], op0=ALU.add, op1=ALU.subtract)
            nc.vector.scalar_tensor_tensor(out=high_key[:], in0=parts[:, 1, :], scalar=float(U),
                                           in1=parts[:, 2, :], op0=ALU.mult, op1=ALU.add)
            dve.drain()
            nc.vector.tensor_tensor(tail_diff[:, 0, :], tail_diff[:, 0, :], in_tail, ALU.mult)
            nc.vector.tensor_scalar(tail_diff[:, 1, :], high_key[:], -1.0, float(HI - 1), ALU.mult, ALU.add)
            dve.drain()
            nc.vector.tensor_tensor(low[:], parts[:, 0, :], tail_diff[:, 0, :], ALU.add)
            nc.vector.tensor_tensor(tail_diff[:, 1, :], tail_diff[:, 1, :], in_tail, ALU.mult)
            dve.drain()
            nc.vector.tensor_tensor(high_key[:], high_key[:], tail_diff[:, 1, :], ALU.add)
            dve.drain()
            for run in PLAN:
                keys = high_key[:, run.head0 * U:(run.head0 + run.n * run.hs) * U]
                nc.vector.tensor_scalar(keys, keys, float(run.hw), 1.0, ALU.mult, ALU.add)
            dve.drain()
            nc.vector.tensor_tensor(pair_key[:], dst_rel[:, 0:HT], high_key[:], ALU.add)
            dve.drain()
            for run in PLAN:
                t0, t1 = run.head0 * U, (run.head0 + run.n * run.hs) * U
                nc.vector.scalar_tensor_tensor(out=pair_key[:, t0:t1], in0=dst_rel[:, t0:t1], scalar=float(run.hw),
                                               in1=pair_key[:, t0:t1], op0=ALU.is_lt, op1=ALU.mult)
            dve.drain()
            nc.vector.tensor_scalar(pair_key[:], pair_key[:], -1.0, None, ALU.add).then_inc(tables_ready, 1)
            dve.wait_ge(tables_ready, 1)
            dve.wait_ge(head_consts_ready, 1)

            more_count = dve.alloc_register("dve_more_count")
            dve.reg_mov(more_count, 0)
            head_count = dve.alloc_register("dve_head_count")
            dve.reg_mov(head_count, 0)

            def build_onehot(g, p):
                nc.vector.tensor_tensor(
                    onehot[:, p % HOTS, :].rearrange("p (u n) -> p u n", u=U),
                    iota_sb[:].unsqueeze(1).to_broadcast([P, U, WIN]),
                    dst_rel[:, bass.ds(g * U, U)].unsqueeze(2).to_broadcast([P, U, WIN]),
                    ALU.is_equal).then_inc(onehot_ready, 1)

            def hot_pair(run, tile, key, lo):
                nc.vector.tensor_scalar(low_hot[:, tile % run.ring, :], iota_lo[:], lo, None, ALU.is_equal)
                return nc.vector.tensor_scalar(pair_buffer(run, tile), iota_z[:, 0:HI * run.hw], key, None,
                                               ALU.is_equal)

            def build_pair(run, i, tile):
                t = (run.head0 + i * run.hs) * U + tile
                hot_pair(run, tile, pair_key[:, bass.ds(t, 1)], low[:, bass.ds(t, 1)]).then_inc(pair_ready, 1)

            def add_sums(base, sums, width, before):
                dve.wait_ge(added, before)
                nc.vector.tensor_tensor(accT[:, bass.ds(base, width)], accT[:, bass.ds(base, width)],
                                        sums, ALU.add).then_inc(added, 1)

            def base_of(g):
                return dve.value_load(base_i[0:1, bass.ds(g, 1)], min_val=0, max_val=N - 1)

            def bases_of(table, g, n):
                _, values = nc.values_load_multi_w_load_instructions(
                    table[0:1, bass.ds(g, n)], engines=[mybir.EngineType.DVE], min_val=0, max_val=N - 1,
                    skip_runtime_bounds_check_because="they are the lowest of valid destinations")
                return values

            def add_group(g, slot, pos, p, base, before, quick, more=None):
                dve.wait_ge(sum_ready, pos + 1)
                add_sums(base, sums_of(p), WIN, before)
                if not quick:
                    group_windows(g, base, more_of(g) if more is None else more)
                dve.sem_inc(slot_free[slot], 1)

            def more_of(g):
                return dve.value_load(more_i[0:1, bass.ds(g, 1)], min_val=0, max_val=(N - 1) // WIN)

            def group_windows(g, base, more):
                with dve.If(more > 0):
                    nc.vector.tensor_copy(rel_more[:], dst_rel[:, bass.ds(g * U, U)])
                    with dve.Fori(0, more) as k:
                        dve.drain()
                        nc.vector.tensor_scalar(rel_more[:], rel_more[:], -float(WIN), None, ALU.add)
                        dve.drain()
                        for u in range(U):
                            last = nc.vector.tensor_scalar(onehot_more[:, u * WIN:(u + 1) * WIN],
                                                           iota_sb[:], rel_more[:, u:u + 1], None,
                                                           ALU.is_equal)
                        last.then_inc(more_onehot_ready, 1)
                        dve.reg_add(more_count, more_count, 1)
                        at = nc.s_assert_within(dve.snap(base + k * WIN + WIN), 0, N - 1)
                        dve.wait_ge(more_sum_ready, dve.snap(more_count))
                        nc.vector.tensor_tensor(accT[:, bass.ds(at, WIN)], accT[:, bass.ds(at, WIN)],
                                                extra_ps[:, 0:WIN], ALU.add)
                    dve.drain()

            def further_windows(run, i):
                hw, head = run.hw, run.head0 + i * run.hs
                with dve.Fori(0, run.hs) as k:
                    more = dve.value_load(head_more_i[0:1, bass.ds(head + k, 1)], min_val=0, max_val=MORE_MAX)
                    base = dve.value_load(base_i[0:1, bass.ds(head + k, 1)], min_val=0, max_val=N - 1)
                    with dve.If(more > 0):
                        dve.drain()
                        nc.vector.tensor_copy(dst_more[:], dst_rel[:, bass.ds((head + k) * U, U)])
                        with dve.Fori(0, more) as w:
                            dve.drain()
                            nc.vector.tensor_scalar(dst_more[:], dst_more[:], -float(hw), None, ALU.add)
                            dve.drain()
                            nc.vector.tensor_scalar(in_more[:], dst_more[:], 0.0, None, ALU.is_ge)
                            nc.vector.tensor_tensor(key_more[:], dst_more[:], high_key[:, bass.ds((head + k) * U, U)],
                                                    ALU.add)
                            dve.drain()
                            nc.vector.scalar_tensor_tensor(out=key_more[:], in0=dst_more[:], scalar=float(hw),
                                                           in1=key_more[:], op0=ALU.is_lt, op1=ALU.mult)
                            dve.drain()
                            nc.vector.tensor_tensor(key_more[:], key_more[:], in_more[:], ALU.mult)
                            dve.drain()
                            nc.vector.tensor_scalar(key_more[:], key_more[:], -1.0, None, ALU.add)
                            dve.drain()
                            dve.wait_ge(counted, (head + run.hs) * U)
                            for u in range(U):
                                last = hot_pair(run, u, key_more[:, u:u + 1], low[:, bass.ds((head + k) * U + u, 1)])
                            last.then_inc(more_pair_ready, 1)
                            dve.reg_add(head_count, head_count, 1)
                            at = nc.s_assert_within(dve.snap(base + w * hw + hw), 0, N - 1 + 2 * hw)
                            dve.wait_ge(more_window_ready, dve.snap(head_count))
                            nc.vector.tensor_tensor(accT[:, bass.ds(at, hw)], accT[:, bass.ds(at, hw)],
                                                    extra_ps[:, 0:hw], ALU.add)
                dve.drain()

            def take_off_second(k):
                nc.vector.tensor_tensor(piece(h_last, k), piece(h_left, k), upper_half(h_left, k * PW, (k + 1) * PW),
                                        ALU.subtract).then_inc(last_ready, 1)

            def head_round(run, i, quick):
                it = run.round0 + i
                is_first = isinstance(i, int) and i == 0
                begin = is_first and run is PLAN[0]
                last_run = PLAN[PLAN.index(run) - 1] if is_first else run
                last_heads = run.before_hs if is_first else run.hs
                bases = {slot: base for slot, base in enumerate(bases_of(other_base_i, it * S, run.s))}
                head_bases = bases_of(base_i, run.head0 + i * run.hs, run.hs)
                last_bases = bases_of(base_i, run.head0 + i * run.hs - last_heads, last_heads) if last_heads else []
                before, adds = adds_before(run, i), 0
                steps = list(places(run, i))

                def add(step):
                    p, k, slot, _, g = step
                    add_group(g, slot, run.pos0 + i * run.q + p, p,
                              bases[slot] if k is None else head_bases[k], before + adds, quick)

                for p, k, slot, _, g in steps:
                    if W0 <= p < W0 + last_heads:
                        at, w = p - W0, last_run.hw
                        if at == 0:
                            dve.wait_ge(window_ready, it)
                        add_sums(last_bases[at], win_ps[:, at * w:(at + 1) * w], w, before + adds)
                        adds += 1
                    if not by_scalar(run, p):
                        build_onehot(g, p)
                    if p >= LAG:
                        add(steps[p - LAG])
                        adds += 1
                    k, *us = run.tiles[p]
                    for two in (us[:2], us[2:]):
                        if two:
                            tile = k * U + two[-1]
                            used = ((run.head0 + i * run.hs) * U + tile + 1 - run.ring
                                    if not is_first or tile >= run.ring else run.head0 * U)
                            if not isinstance(used, int) or used > 0:
                                dve.wait_ge(counted, used)
                            for u in two:
                                build_pair(run, i, k * U + u)
                    if begin and p % 2:
                        if p == 1:
                            dve.wait_ge(left_ready, NP)
                        if p // 2 < NP:
                            take_off_second(p // 2)
                for step in steps[-LAG:]:
                    add(step)
                    adds += 1
                if not quick:
                    further_windows(run, i)

            def any_round(run, i):
                more = dve.value_load(head_more_i[0:1, bass.ds(HG + run.round0 + i, 1)], min_val=0, max_val=MORE_MAX)
                with dve.If(more > 0):
                    head_round(run, i, False)
                with dve.Else():
                    head_round(run, i, True)

            for k in range(EARLY, NP):
                take_off_first(k)
            dve.wait_ge(acc_started, NC + 1)
            for run in PLAN:
                any_round(run, 0)
                if run.n > 1:
                    with dve.Fori(1, run.n) as i:
                        any_round(run, i)
            adds, run = ADDS, PLAN[-1]

            def add_of_tail(t):
                slot, _, g = TAIL[t]
                add_group(g, slot, POS + t, t, tail_bases[t], adds, False, tail_more[t])

            for t, (slot, _, g) in enumerate(TAIL):
                build_onehot(g, t)
                if t == LAG:
                    head_bases = bases_of(base_i, HG - run.hs, run.hs)
                    tail_bases = [base_of(g) for _, _, g in TAIL]
                    tail_more = [more_of(g) for _, _, g in TAIL]
                    dve.wait_ge(window_ready, HR)
                    for k in range(run.hs):
                        add_sums(head_bases[k], win_ps[:, k * run.hw:(k + 1) * run.hw], run.hw, adds)
                        adds += 1
                if t >= LAG:
                    add_of_tail(t - LAG)
                    adds += 1
            for t in range(len(TAIL) - LAG, len(TAIL)):
                add_of_tail(t)
                adds += 1
            dve.drain().then_inc(acc_done, 1)

            def leaky_relu(s, nth, n):
                dve.wait_ge(biased_ready[s], nth)
                if not first(nth):
                    dve.wait_ge(y_ps_ready[s], nth - 1)
                nc.vector.scalar_tensor_tensor(out=hidT[:, s, 0:n], in0=biased[:, s, 0:n], scalar=0.01,
                                               in1=biased[:, s, 0:n], op0=ALU.mult,
                                               op1=ALU.max).then_inc(hid_ready[s], 1)

            def finish(c, s, nth, n, w):
                dve.wait_ge(y_ps_ready[s], nth)
                if not first(nth):
                    dve.wait_ge(y_stored[s], 16 * (nth - 1))
                dve.wait_ge(xb_ready, c + 1)
                nc.vector.tensor_tensor(y_sb[0:n, s, 0:w], sum_ps[s][0:n, 0:w],
                                        x_all[0:n, bass.ds(c * G, w)], ALU.add).then_inc(y_ready[s], 1)

            def finish_pair(j):
                leaky_relu(1, j + 1, G)
                finish(j * 2, 0, j + 1, P, G)
                leaky_relu(0, j + 2, G)
                finish(j * 2 + 1, 1, j + 1, P, G)

            leaky_relu(0, 1, G)
            finish_pair(0)
            with dve.Fori(1, NC // 2) as j:
                finish_pair(j)
            finish(NC, 0, NC // 2 + 1, NT, D)

        @block.tensor
        def _(pe):
            pe.wait_ge(ident_ready, 1)

            def turn_rows(table, halves):
                for half in range(2):
                    for u in range(U):
                        last = nc.tensor.transpose(halves[half][:, u * NH:(u + 1) * NH], table[:, half, u:G:U],
                                                   ident[0:NH, 0:NH])
                return last

            pe.wait_ge(src_floats, 1)
            turn_rows(src_f, src_ps).then_inc(src_turned, 1)
            pe.wait_ge(dst_floats, 1)
            turn_rows(dst_f, dst_ps).then_inc(dst_turned, 1)
            pe.wait_ge(consts_ready, 1)
            pe.wait_ge(diags_ready, 1)
            nc.tensor.matmul(row_ps[:, 0:2 * NH], ones[0:NH, :], lo_diag[:].rearrange("k a g -> k (a g)"),
                             start=True, stop=True)
            nc.tensor.matmul(row_ps[:, 2 * NH:4 * NH], ones[0:NH, :], spread_diag[:].rearrange("k a g -> k (a g)"),
                             start=True, stop=True).then_inc(rows_ready, 1)

            pe.wait_ge(spread_copied, 1)
            for c in range(NC):
                if c % CL < CL - 1:
                    pe.wait_ge(h_ready, c // CL * (CL - 1) + c % CL + 1)
                else:
                    pe.wait_ge(h_ready_pool, c // CL + 1)
                if c >= 2:
                    pe.wait_ge(acc_started, c - 1)
                for u in range(U):
                    last = nc.tensor.transpose(turn_ps[c % 2][:, u * P:(u + 1) * P],
                                               h_all[:, c * G + u * D:c * G + (u + 1) * D], ident[:])
                last.then_inc(hT_ready, 1)
            pe.wait_ge(h_ready, LOADS * (CL - 1) + 1)
            pe.wait_ge(acc_started, NC - 1)
            nc.tensor.transpose(turn_ps[0][:, 0:NT], h_all[0:NT, NC * G:NC * G + D],
                                ident[0:NT, 0:NT]).then_inc(hT_ready, 1)
            pe.wait_ge(src_all_ready, 1)
            pe.wait_ge(base_copied, 1)
            pe.wait_ge(acc_started, NC + 1)

            pe.wait_ge(tables_ready, 1)
            more_count = pe.alloc_register("pe_more_count")
            pe.reg_mov(more_count, 0)

            head_count = pe.alloc_register("pe_head_count")
            pe.reg_mov(head_count, 0)

            def sum_slot(into, hot, slot, p1):
                for u in range(U):
                    last = nc.tensor.matmul(into[:, 0:WIN], edges[0:p1, slot, u * D:(u + 1) * D],
                                            hot[0:p1, u * WIN:(u + 1) * WIN],
                                            start=(u == 0), stop=(u == U - 1))
                return last

            def sum_group(g, slot, nth, hot_sem, hots, p, p1=P, quick=False):
                more = None if quick else pe.value_load(more_i[0:1, bass.ds(g, 1)], min_val=0, max_val=(N - 1) // WIN)
                pe.wait_ge(hot_sem, hots)
                if slot < S:
                    pe.wait_ge(rows_gathered[slot], 16 * U * nth)
                else:
                    pe.wait_ge(edges_loaded[slot], 16 * nth)
                sum_slot(sums_of(p), onehot[:, p % HOTS, :], slot, p1).then_inc(sum_ready, 1)
                if quick:
                    return
                with pe.If(more > 0):
                    with pe.Fori(0, more):
                        pe.reg_add(more_count, more_count, 1)
                        pe.wait_ge(more_onehot_ready, pe.snap(more_count))
                        sum_slot(extra_ps, onehot_more[:], slot, p1).then_inc(more_sum_ready, 1)

            def count_pairs(run, tile):
                for c in range(0, HI * run.hw, 512):
                    w = min(512, HI * run.hw - c)
                    last = nc.tensor.matmul(a_ps[:, c:c + w], low_hot[:, tile % run.ring, :],
                                            pair_buffer(run, tile)[:, c:c + w],
                                            start=(tile % U == 0), stop=True, skip_group_check=True)
                return last

            def window_product(run, into, heads):
                for t in range(HI):
                    parts_of_h = (upper_half(h_all, t * D, (t + 1) * D), upper_half(h_left, t * D, (t + 1) * D),
                                  h_last[:, t * D:(t + 1) * D])
                    for k, part in enumerate(parts_of_h):
                        last = nc.tensor.matmul(into[:, 0:heads * run.hw], part,
                                                run_counts(run)[:, t, 0:heads, :],
                                                start=(t == 0 and k == 0), stop=(t == HI - 1 and k == 2))
                return last

            def further_windows(run, i):
                with pe.Fori(0, run.hs) as k:
                    more = pe.value_load(head_more_i[0:1, bass.ds(run.head0 + i * run.hs + k, 1)],
                                         min_val=0, max_val=MORE_MAX)
                    with pe.If(more > 0):
                        with pe.Fori(0, more):
                            pe.reg_add(head_count, head_count, 1)
                            pe.wait_ge(more_pair_ready, pe.snap(head_count))
                            for u in range(U):
                                last = count_pairs(run, u)
                            last.then_inc(more_counted, 1)
                            pe.wait_ge(more_copied, pe.snap(head_count))
                            window_product(run, extra_ps, 1).then_inc(more_window_ready, 1)

            def sum_and_count(run, i, quick):
                for p, _, slot, nth, g in places(run, i):
                    if by_scalar(run, p):
                        hot_sem = act_onehot_ready
                        hots = (i * act_hots(run)
                                + (act_hots_before(run) + sum(by_scalar(run, at) for at in range(p + 1))))
                    else:
                        hot_sem, hots = onehot_ready, hots_before(run, i, p) + 1
                    sum_group(g, slot, nth, hot_sem, hots, p, quick=quick)
                    k, *us = run.tiles[p]
                    head = run.head0 + i * run.hs + k
                    for u in us:
                        pe.wait_ge(pair_ready, head * U + u + 1)
                        if u == 0 and k:
                            pe.wait_ge(counts_copied, head)
                        count_pairs(run, k * U + u).then_inc(counted, 1)

            def heads_product(run, i):
                pe.wait_ge(last_ready, NP)
                pe.wait_ge(counts_copied, run.head0 + (i + 1) * run.hs)
                pe.wait_ge(added, (i + 1) * (run.q + run.hs) + (run.adds0 + run.before_hs - run.hs - LAG))
                window_product(run, win_ps, run.hs).then_inc(window_ready, 1)

            for run in PLAN:
                with pe.Fori(0, run.n) as i:
                    more = pe.value_load(head_more_i[0:1, bass.ds(HG + run.round0 + i, 1)], min_val=0, max_val=MORE_MAX)
                    with pe.If(more > 0):
                        sum_and_count(run, i, False)
                        heads_product(run, i)
                        further_windows(run, i)
                    with pe.Else():
                        sum_and_count(run, i, True)
                        heads_product(run, i)
            for t, (slot, nth, g) in enumerate(TAIL):
                sum_group(g, slot, nth, onehot_ready, hots_before(PLAN[-1], 1, t) + 1, t, PT if g == NG else P)

            pe.wait_ge(acc_done, 1)
            pe.wait_ge(weights_loaded, 64)

            def first_layer(c, s, nth):
                if not first(nth):
                    pe.wait_ge(biased_ready[s], nth - 1)
                nc.tensor.matmul(wide_ps[s], w1_sb[:], accT[:, bass.ds(c * G, G)],
                                 start=True, stop=True).then_inc(wide_ready[s], 1)

            def second_layer(s, nth, tiles):
                pe.wait_ge(hid_ready[s], nth)
                if not first(nth):
                    pe.wait_ge(y_ready[s], nth - 1)
                for at, (n, nodes) in enumerate(tiles):
                    last = nc.tensor.matmul(sum_ps[s][0:n, at * D:(at + 1) * D], nodes, w2_sb[:],
                                            start=True, stop=True)
                last.then_inc(y_ps_ready[s], 1)

            def tiles_of(s):
                return [(P, hidT[:, s, u:G:U]) for u in range(U)]

            def layer_pair(j):
                first_layer(j * 2 + 1, 1, j + 1)
                second_layer(0, j + 1, tiles_of(0))
                first_layer(j * 2 + 2, 0, j + 2)
                second_layer(1, j + 1, tiles_of(1))

            first_layer(0, 0, 1)
            layer_pair(0)
            with pe.Fori(1, NC // 2) as j:
                layer_pair(j)
            second_layer(0, NC // 2 + 1, [(NT, hidT[:, 0, 0:NT])])


_INS = ["x", "src", "dst", "edge_attr_128", "L0_gnn_W1", "L0_gnn_b1", "L0_gnn_W2", "L0_gnn_b2"]


def kernel(**inputs):
    import numpy as _np
    import concourse.bacc as _bacc
    from concourse import mybir as _mybir
    from concourse.bass_utils import run_bass_kernel_spmd as _run

    nc = _bacc.Bacc("TRN2", target_bir_lowering=False, num_devices=1)
    arrays, args = {}, []
    for name in _INS:
        a = _np.ascontiguousarray(inputs[name])
        arrays[f"in_{name}"] = a
        args.append(nc.dram_tensor(f"in_{name}", a.shape, _mybir.dt.from_np(a.dtype), kind="ExternalInput").ap())
    shape = inputs["x"].shape
    args.append(nc.dram_tensor("out_0", shape, _mybir.dt.float32, kind="ExternalOutput").ap())
    gnn_preln_kernel(nc, *args)
    r = _run(nc, [arrays], core_ids=[0])
    return r.results[0]["out_0"]
```
